# Optimizing a Trainium2 kernel written in Bass

```python
import numpy as np
import jax
import jax.numpy as jnp

def _softmax(x, axis=-1):
    return jax.nn.softmax(x, axis=axis)

def _gelu(x):
    return jax.nn.gelu(x, approximate=True)

def _silu(x):
    return jax.nn.silu(x)

def _sigmoid(x):
    return jax.nn.sigmoid(x)

def _layernorm(x, axis=-1, eps=1e-05):
    m = jnp.mean(x, axis=axis, keepdims=True)
    v = jnp.var(x, axis=axis, keepdims=True)
    return (x - m) / jnp.sqrt(v + eps)

def _scatter_add(tgt, idx, src, axis=0):
    return tgt.at[idx].add(src)

def _segment_sum(src, seg, n):
    return jax.ops.segment_sum(src, seg, n)
kernel_name = 'mk_dlrm_tower_d1_rec_r8_a4d2d5'

def setup_inputs(seed: int=0):
    np.random.seed(seed)
    _w = jnp.asarray

    def _rec_inputs():
        import jax
        import jax.numpy as jnp
        _tk = jax.random.key(seed)
        dense_ctx = jax.random.normal(jax.random.fold_in(_tk, 190), (1024, 16), jnp.float32)
        ids = jnp.stack([jax.random.randint(jax.random.fold_in(_tk, 200 + f), (1024,), 0, v, jnp.int32) for f, v in enumerate([125000, 12500, 125000, 125000, 1250, 1000, 1250, 125000, 1000, 1250, 1000, 125000, 125000, 1000, 125000, 125000, 1250, 125000, 1000, 12500, 125000, 125000, 12500, 125000, 1250, 12500, 1000, 1000, 12500, 1000, 1250, 12500, 1250, 1000, 1000, 12500, 1000, 125000, 1250])], axis=1)
        tbl_0 = 0.05 * jax.random.normal(jax.random.fold_in(_tk, 500 + 0), (125000, 16), jnp.float32)
        tbl_1 = 0.05 * jax.random.normal(jax.random.fold_in(_tk, 500 + 1), (12500, 16), jnp.float32)
        tbl_2 = 0.05 * jax.random.normal(jax.random.fold_in(_tk, 500 + 2), (125000, 16), jnp.float32)
        tbl_3 = 0.05 * jax.random.normal(jax.random.fold_in(_tk, 500 + 3), (125000, 16), jnp.float32)
        tbl_4 = 0.05 * jax.random.normal(jax.random.fold_in(_tk, 500 + 4), (1250, 16), jnp.float32)
        tbl_5 = 0.05 * jax.random.normal(jax.random.fold_in(_tk, 500 + 5), (1000, 16), jnp.float32)
        tbl_6 = 0.05 * jax.random.normal(jax.random.fold_in(_tk, 500 + 6), (1250, 16), jnp.float32)
        tbl_7 = 0.05 * jax.random.normal(jax.random.fold_in(_tk, 500 + 7), (125000, 16), jnp.float32)
        tbl_8 = 0.05 * jax.random.normal(jax.random.fold_in(_tk, 500 + 8), (1000, 16), jnp.float32)
        tbl_9 = 0.05 * jax.random.normal(jax.random.fold_in(_tk, 500 + 9), (1250, 16), jnp.float32)
        tbl_10 = 0.05 * jax.random.normal(jax.random.fold_in(_tk, 500 + 10), (1000, 16), jnp.float32)
        tbl_11 = 0.05 * jax.random.normal(jax.random.fold_in(_tk, 500 + 11), (125000, 16), jnp.float32)
        tbl_12 = 0.05 * jax.random.normal(jax.random.fold_in(_tk, 500 + 12), (125000, 16), jnp.float32)
        tbl_13 = 0.05 * jax.random.normal(jax.random.fold_in(_tk, 500 + 13), (1000, 16), jnp.float32)
        tbl_14 = 0.05 * jax.random.normal(jax.random.fold_in(_tk, 500 + 14), (125000, 16), jnp.float32)
        tbl_15 = 0.05 * jax.random.normal(jax.random.fold_in(_tk, 500 + 15), (125000, 16), jnp.float32)
        tbl_16 = 0.05 * jax.random.normal(jax.random.fold_in(_tk, 500 + 16), (1250, 16), jnp.float32)
        tbl_17 = 0.05 * jax.random.normal(jax.random.fold_in(_tk, 500 + 17), (125000, 16), jnp.float32)
        tbl_18 = 0.05 * jax.random.normal(jax.random.fold_in(_tk, 500 + 18), (1000, 16), jnp.float32)
        tbl_19 = 0.05 * jax.random.normal(jax.random.fold_in(_tk, 500 + 19), (12500, 16), jnp.float32)
        tbl_20 = 0.05 * jax.random.normal(jax.random.fold_in(_tk, 500 + 20), (125000, 16), jnp.float32)
        tbl_21 = 0.05 * jax.random.normal(jax.random.fold_in(_tk, 500 + 21), (125000, 16), jnp.float32)
        tbl_22 = 0.05 * jax.random.normal(jax.random.fold_in(_tk, 500 + 22), (12500, 16), jnp.float32)
        tbl_23 = 0.05 * jax.random.normal(jax.random.fold_in(_tk, 500 + 23), (125000, 16), jnp.float32)
        tbl_24 = 0.05 * jax.random.normal(jax.random.fold_in(_tk, 500 + 24), (1250, 16), jnp.float32)
        tbl_25 = 0.05 * jax.random.normal(jax.random.fold_in(_tk, 500 + 25), (12500, 16), jnp.float32)
        tbl_26 = 0.05 * jax.random.normal(jax.random.fold_in(_tk, 500 + 26), (1000, 16), jnp.float32)
        tbl_27 = 0.05 * jax.random.normal(jax.random.fold_in(_tk, 500 + 27), (1000, 16), jnp.float32)
        tbl_28 = 0.05 * jax.random.normal(jax.random.fold_in(_tk, 500 + 28), (12500, 16), jnp.float32)
        tbl_29 = 0.05 * jax.random.normal(jax.random.fold_in(_tk, 500 + 29), (1000, 16), jnp.float32)
        tbl_30 = 0.05 * jax.random.normal(jax.random.fold_in(_tk, 500 + 30), (1250, 16), jnp.float32)
        tbl_31 = 0.05 * jax.random.normal(jax.random.fold_in(_tk, 500 + 31), (12500, 16), jnp.float32)
        tbl_32 = 0.05 * jax.random.normal(jax.random.fold_in(_tk, 500 + 32), (1250, 16), jnp.float32)
        tbl_33 = 0.05 * jax.random.normal(jax.random.fold_in(_tk, 500 + 33), (1000, 16), jnp.float32)
        tbl_34 = 0.05 * jax.random.normal(jax.random.fold_in(_tk, 500 + 34), (1000, 16), jnp.float32)
        tbl_35 = 0.05 * jax.random.normal(jax.random.fold_in(_tk, 500 + 35), (12500, 16), jnp.float32)
        tbl_36 = 0.05 * jax.random.normal(jax.random.fold_in(_tk, 500 + 36), (1000, 16), jnp.float32)
        tbl_37 = 0.05 * jax.random.normal(jax.random.fold_in(_tk, 500 + 37), (125000, 16), jnp.float32)
        tbl_38 = 0.05 * jax.random.normal(jax.random.fold_in(_tk, 500 + 38), (1250, 16), jnp.float32)
        _rk = jax.random.fold_in(_tk, 7)
        W_top1 = 0.05 * jax.random.normal(jax.random.fold_in(_tk, 801), (400, 512), jnp.float32)
        W_top2 = 0.0441942 * jax.random.normal(jax.random.fold_in(_tk, 802), (512, 256), jnp.float32)
        W_top3 = 0.0625 * jax.random.normal(jax.random.fold_in(_tk, 803), (256, 1), jnp.float32)
        b_top1 = jnp.zeros((512,), jnp.float32)
        b_top2 = jnp.zeros((256,), jnp.float32)
        return (dense_ctx, ids, tbl_0, tbl_1, tbl_2, tbl_3, tbl_4, tbl_5, tbl_6, tbl_7, tbl_8, tbl_9, tbl_10, tbl_11, tbl_12, tbl_13, tbl_14, tbl_15, tbl_16, tbl_17, tbl_18, tbl_19, tbl_20, tbl_21, tbl_22, tbl_23, tbl_24, tbl_25, tbl_26, tbl_27, tbl_28, tbl_29, tbl_30, tbl_31, tbl_32, tbl_33, tbl_34, tbl_35, tbl_36, tbl_37, tbl_38, W_top1, b_top1, W_top2, b_top2, W_top3)
    dense_ctx, ids, tbl_0, tbl_1, tbl_2, tbl_3, tbl_4, tbl_5, tbl_6, tbl_7, tbl_8, tbl_9, tbl_10, tbl_11, tbl_12, tbl_13, tbl_14, tbl_15, tbl_16, tbl_17, tbl_18, tbl_19, tbl_20, tbl_21, tbl_22, tbl_23, tbl_24, tbl_25, tbl_26, tbl_27, tbl_28, tbl_29, tbl_30, tbl_31, tbl_32, tbl_33, tbl_34, tbl_35, tbl_36, tbl_37, tbl_38, W_top1, b_top1, W_top2, b_top2, W_top3 = _rec_inputs()

    def _L0_rec_setup():
        import jax, jax.numpy as jnp
        import numpy as np
        B, F0, D = (512, 39, 16)
        CIN = [128, 128, 128]

        def _cin_layer(X0, Xi, W, b):
            H = W.shape[0]
            F0_, Fi = (X0.shape[1], Xi.shape[1])
            Wr = W.reshape(H, F0_, Fi)
            return jnp.einsum('hjk,bjd,bkd->bhd', Wr, X0, Xi) + b[None, :, None]
        key = jax.random.key(seed)
        ks = jax.random.split(key, 4)
        x = jax.random.normal(ks[0], (B, F0, D), dtype=jnp.float32)
        fields = [F0] + CIN
        inp = {'embedded_features': x}
        for i in range(len(CIN)):
            cin = F0 * fields[i]
            cout = fields[i + 1]
            kw = jax.random.fold_in(ks[1], i)
            inp[f'W{i}'] = jax.random.normal(kw, (cout, cin), dtype=jnp.float32) / np.sqrt(cin)
            inp[f'b{i}'] = jnp.zeros((cout,), dtype=jnp.float32)
        return inp
    _L0_rec_all = _L0_rec_setup()
    _L0_rec_in = {k: v for k, v in _L0_rec_all.items() if k in ('W0', 'b0', 'W1', 'b1', 'W2', 'b2')}
    del _L0_rec_all
    return {'dense_ctx': dense_ctx, 'ids': ids, 'tbl_0': tbl_0, 'tbl_1': tbl_1, 'tbl_2': tbl_2, 'tbl_3': tbl_3, 'tbl_4': tbl_4, 'tbl_5': tbl_5, 'tbl_6': tbl_6, 'tbl_7': tbl_7, 'tbl_8': tbl_8, 'tbl_9': tbl_9, 'tbl_10': tbl_10, 'tbl_11': tbl_11, 'tbl_12': tbl_12, 'tbl_13': tbl_13, 'tbl_14': tbl_14, 'tbl_15': tbl_15, 'tbl_16': tbl_16, 'tbl_17': tbl_17, 'tbl_18': tbl_18, 'tbl_19': tbl_19, 'tbl_20': tbl_20, 'tbl_21': tbl_21, 'tbl_22': tbl_22, 'tbl_23': tbl_23, 'tbl_24': tbl_24, 'tbl_25': tbl_25, 'tbl_26': tbl_26, 'tbl_27': tbl_27, 'tbl_28': tbl_28, 'tbl_29': tbl_29, 'tbl_30': tbl_30, 'tbl_31': tbl_31, 'tbl_32': tbl_32, 'tbl_33': tbl_33, 'tbl_34': tbl_34, 'tbl_35': tbl_35, 'tbl_36': tbl_36, 'tbl_37': tbl_37, 'tbl_38': tbl_38, 'W_top1': W_top1, 'b_top1': b_top1, 'W_top2': W_top2, 'b_top2': b_top2, 'W_top3': W_top3, 'L0_rec_W0': _L0_rec_in['W0'], 'L0_rec_b0': _L0_rec_in['b0'], 'L0_rec_W1': _L0_rec_in['W1'], 'L0_rec_b1': _L0_rec_in['b1'], 'L0_rec_W2': _L0_rec_in['W2'], 'L0_rec_b2': _L0_rec_in['b2']}

def reference(dense_ctx, ids, tbl_0, tbl_1, tbl_2, tbl_3, tbl_4, tbl_5, tbl_6, tbl_7, tbl_8, tbl_9, tbl_10, tbl_11, tbl_12, tbl_13, tbl_14, tbl_15, tbl_16, tbl_17, tbl_18, tbl_19, tbl_20, tbl_21, tbl_22, tbl_23, tbl_24, tbl_25, tbl_26, tbl_27, tbl_28, tbl_29, tbl_30, tbl_31, tbl_32, tbl_33, tbl_34, tbl_35, tbl_36, tbl_37, tbl_38, W_top1, b_top1, W_top2, b_top2, W_top3, L0_rec_W0, L0_rec_b0, L0_rec_W1, L0_rec_b1, L0_rec_W2, L0_rec_b2):
    import jax
    import jax.numpy as jnp

    def _L0_rec_ref(embedded_features, W0, b0, W1, b1, W2, b2):
        import jax, jax.numpy as jnp
        import numpy as np
        B, F0, D = (512, 39, 16)
        CIN = [128, 128, 128]

        def _cin_layer(X0, Xi, W, b):
            H = W.shape[0]
            F0_, Fi = (X0.shape[1], Xi.shape[1])
            Wr = W.reshape(H, F0_, Fi)
            return jnp.einsum('hjk,bjd,bkd->bhd', Wr, X0, Xi) + b[None, :, None]
        X0 = embedded_features
        Ws = [(W0, b0), (W1, b1), (W2, b2)]
        Xi = X0
        res = []
        for W, b in Ws:
            Xi = _cin_layer(X0, Xi, W, b)
            res.append(Xi.sum(axis=2))
        return jnp.concatenate(res, axis=1)
    e = jnp.stack([tbl_0[ids[:, 0]], tbl_1[ids[:, 1]], tbl_2[ids[:, 2]], tbl_3[ids[:, 3]], tbl_4[ids[:, 4]], tbl_5[ids[:, 5]], tbl_6[ids[:, 6]], tbl_7[ids[:, 7]], tbl_8[ids[:, 8]], tbl_9[ids[:, 9]], tbl_10[ids[:, 10]], tbl_11[ids[:, 11]], tbl_12[ids[:, 12]], tbl_13[ids[:, 13]], tbl_14[ids[:, 14]], tbl_15[ids[:, 15]], tbl_16[ids[:, 16]], tbl_17[ids[:, 17]], tbl_18[ids[:, 18]], tbl_19[ids[:, 19]], tbl_20[ids[:, 20]], tbl_21[ids[:, 21]], tbl_22[ids[:, 22]], tbl_23[ids[:, 23]], tbl_24[ids[:, 24]], tbl_25[ids[:, 25]], tbl_26[ids[:, 26]], tbl_27[ids[:, 27]], tbl_28[ids[:, 28]], tbl_29[ids[:, 29]], tbl_30[ids[:, 30]], tbl_31[ids[:, 31]], tbl_32[ids[:, 32]], tbl_33[ids[:, 33]], tbl_34[ids[:, 34]], tbl_35[ids[:, 35]], tbl_36[ids[:, 36]], tbl_37[ids[:, 37]], tbl_38[ids[:, 38]]], axis=1)
    z = _L0_rec_ref(e, L0_rec_W0, L0_rec_b0, L0_rec_W1, L0_rec_b1, L0_rec_W2, L0_rec_b2)
    z = z.reshape(z.shape[0], -1)
    h = jnp.concatenate([z, dense_ctx], axis=1)
    h = jnp.maximum(h @ W_top1 + b_top1, 0.0)
    h = jnp.maximum(h @ W_top2 + b_top2, 0.0)
    y = h @ W_top3
    return y

_drawn_inputs = setup_inputs


def setup_inputs(seed=0):
    import zlib

    import numpy as np

    out = dict(_drawn_inputs(seed))
    spreads = {'b_top1': (0.0, 0.1),
     'b_top2': (0.0, 0.1),
     'L0_rec_b0': (0.0, 0.1),
     'L0_rec_b1': (0.0, 0.1),
     'L0_rec_b2': (0.0, 0.1)}
    factors = {'tbl_0': 8.0,
     'tbl_1': 5.95,
     'tbl_2': 5.292,
     'tbl_3': 6.94,
     'tbl_4': 8.0,
     'tbl_5': 8.0,
     'tbl_6': 8.0,
     'tbl_7': 6.675,
     'tbl_8': 8.0,
     'tbl_9': 8.0,
     'tbl_10': 8.0,
     'tbl_11': 6.498,
     'tbl_12': 8.0,
     'tbl_13': 8.0,
     'tbl_14': 4.382,
     'tbl_15': 5.485,
     'tbl_16': 8.0,
     'tbl_17': 8.0,
     'tbl_18': 8.0,
     'tbl_19': 6.032,
     'tbl_20': 7.159,
     'tbl_21': 8.0,
     'tbl_22': 8.0,
     'tbl_23': 8.0,
     'tbl_24': 8.0,
     'tbl_25': 7.21,
     'tbl_26': 5.699,
     'tbl_27': 8.0,
     'tbl_28': 8.0,
     'tbl_29': 8.0,
     'tbl_30': 6.55,
     'tbl_31': 6.526,
     'tbl_32': 8.0,
     'tbl_33': 6.36,
     'tbl_34': 8.0,
     'tbl_35': 7.126,
     'tbl_36': 8.0,
     'tbl_37': 6.634,
     'tbl_38': 8.0,
     'L0_rec_W0': 3.266}
    for name, (base, spread) in spreads.items():
        noise = np.random.default_rng([zlib.crc32(name.encode()), seed]).standard_normal(out[name].shape)
        drawn = base * np.exp(spread * noise) if base else spread * noise
        out[name] = jnp.asarray(drawn.astype(out[name].dtype))
    for name, factor in factors.items():
        out[name] = (out[name] * factor).astype(out[name].dtype)
    return out
```

```python
import concourse.bass as bass
from concourse import mybir
from contextlib import ExitStack

F32 = mybir.dt.float32
F32R = mybir.dt.float32r
I32 = mybir.dt.int32
ALU = mybir.AluOpType
ACT = mybir.ActivationFunctionType
AX = mybir.AxisListType

P = 128
B = 1024
F = 39
D = 16
H = 128
BT = B // P
DC = 4
CH = D // DC
SHIFTS = (F + 1) // 2
SPT = 3
T0 = -(-SHIFTS // SPT)
FX = F + SHIFTS - 1
JB = 4
NB = -(-F // JB)
HALF = NB // 2
MACS = HALF * JB
PROD_SLOTS = 5
P_SLOTS = 4
X2_SLOTS = 4
NG = P // 8
JX = F + 1
GU = NG + 5
TOP1, TOP2, ND = 512, 256, 16
SLOTS = DC * NB

S_A, S_B, S_MM, S_X1, S_XL, EVERY = 0, 2, 5, 31, 33, 4
S_FIELDS = 22
S_PAIRS = (28, 30, 32, 34)
G_AT = {(0, 21 + 3 * g): g for g in range(6)} | {(1, 1 + 3 * (g - 6)): g for g in range(6, NG)}
DENSE_AT = (1, 33)
W2_AT = {(2, 3 * n): n for n in range(13)}
TOP1_AT, TOP2_AT, TOP3_AT = (3, 3), (3, 13), (3, 18)
DIAG_AT = {(2, 7 + 8 * r): r for r in range(4)}


def transposed_bank_order():
    order = {}
    for c in range(CH):
        steps = [(S_B + EVERY * t, "pair", t) for t in range(T0)]
        steps += [(s, "diag", r) for (cc, s), r in DIAG_AT.items() if cc == c]
        for _, kind, n in sorted(steps):
            order[c, kind, n] = len(order)
    return order


TR_ORDER = transposed_bank_order()
TR_PER_ITER = len(TR_ORDER)


def cin_tower(nc, dense_ctx, ids, tables, W_top1, b_top1, W_top2, b_top2, W_top3,
              W0, b0, W1, b1, W2, b2, out):
    x2_dram = nc.dram_tensor("x2_scratch", (P * D, H), F32, kind="Internal").ap()
    ctx = ExitStack()
    with ctx:
        def sb(name, shape, dt=F32):
            return ctx.enter_context(nc.sbuf_tensor(name, shape, dt))

        def pb(name):
            return ctx.enter_context(nc.psum_tensor(name, [P, 512], F32))

        def sem(name):
            return ctx.enter_context(nc.semaphore(name))

        ident = sb("ident", [P, P])
        mask = sb("mask", [P, 8])
        ids_sb = sb("ids_sb", [P, F], I32)
        e_land = sb("e_land", [P, F, D])
        e_tr = sb("e_tr", [P, D, FX])
        e_sc = sb("e_sc", [P, D, F])
        pairsT = sb("pairsT", [P, DC, SHIFTS * F])
        x0bd = sb("x0bd", [F, P, D])
        pairs = sb("pairs", [SPT * F, P_SLOTS, 512])
        w0s = pairsT[:, 0, :]
        w0T = sb("w0T", [SPT * F, T0, H])
        x1f = sb("x1f", [P, 2, 512])
        x1hi = sb("x1hi", [P, CH, 512], F32R)
        x1lo = sb("x1lo", [P, CH, 512], F32R)
        z0part = sb("z0part", [P, CH, P])
        w1hi = sb("w1hi", [P, F * H], F32R)
        w1lo = sb("w1lo", [P, F * H], F32R)
        w2T = sb("w2T", [P, F, H])
        prods = sb("prods", [P, PROD_SLOTS, JB * H])
        acc = sb("acc", [P, 2, 2, H])
        ab = sb("ab", [P, 2, H])
        psum4 = sb("psum4", [P, JB * H])
        psum2 = sb("psum2", [P, 2 * H])
        psum1 = sb("psum1", [P, H])
        x2t = sb("x2t", [P, X2_SLOTS, H])
        x2g = sb("x2g", [P, NG, H])
        diag = sb("diag", [P, NG, 8, JX])
        gram = sb("gram", [P, JX, P])
        w1raw = gram[:, :, :].rearrange("p j b -> p (j b)")
        w2raw = diag[:, :, :, :].rearrange("p g b j -> p (g b j)")
        W0N = (FX + 1) * F
        w0x = w2raw[:, 0:W0N]
        w0y = w2raw[:, W0N:2 * W0N]
        b0c = sb("b0c", [P, 1])
        b1rep = sb("b1rep", [P, H])
        b2c = sb("b2c", [P, 1])
        b2sum = sb("b2sum", [P, 1])
        bt1 = sb("bt1", [P, TOP1 // P])
        bt2 = sb("bt2", [P, TOP2 // P])
        wt1 = sb("wt1", [P, 3, TOP1])
        wt1d = sb("wt1d", [ND, TOP1])
        wt2 = sb("wt2", [P, TOP1 // P, TOP2])
        wt3 = sb("wt3", [P, TOP2 // P])
        z0T = sb("z0T", [P, P])
        z2T = sb("z2T", [P, P])
        dn = sb("dn", [P, ND])
        dnT = sb("dnT", [ND, P])
        h1T = sb("h1T", [P, TOP1 // P, P])
        h2T = sb("h2T", [P, TOP2 // P, P])
        y_sb = sb("y_sb", [1, P])

        yd = [pb("yd0"), pb("yd1")]
        ya = [pb("ya0"), pb("ya1")]
        tr = [pb("tr0"), pb("tr1")]
        l0 = pb("l0")
        tail = pb("tail")

        consts_done = sem("consts_done")
        w0_loaded = sem("w0_loaded")
        w1_loaded = sem("w1_loaded")
        w2_loaded = sem("w2_loaded")
        small_loaded = sem("small_loaded")
        w0_summed = sem("w0_summed")
        wtr = sem("wtr")
        w_hi = sem("w_hi")
        w_lo = sem("w_lo")
        setup_done = sem("setup_done")
        ids_loaded = sem("ids_loaded")
        gathered = sem("gathered")
        e_copied = sem("e_copied")
        x0_tr = sem("x0_tr")
        x0_out = sem("x0_out")
        pairs_made = sem("pairs_made")
        tr_ready = sem("tr_ready")
        tr_done = sem("tr_done")
        l0_mm = sem("l0_mm")
        x1_out = sem("x1_out")
        x1_split = sem("x1_split")
        z0_done = sem("z0_done")
        yd_ready = sem("yd_ready")
        ya_ready = sem("ya_ready")
        macs = sem("macs")
        ab_ready = sem("ab_ready")
        prods_ready = sem("prods_ready")
        prods_added = sem("prods_added")
        folded = sem("folded")
        x2_ready = sem("x2_ready")
        x2_stored = [sem(f"x2_stored{n}") for n in range(X2_SLOTS)]
        x2_loaded = sem("x2_loaded")
        dense_loaded = sem("dense_loaded")
        tail_ready = sem("tail_ready")
        tail_done = sem("tail_done")
        y_free = sem("y_free")

        block = ctx.enter_context(nc.Block())

        def wait(eng, s, value):
            if not isinstance(value, int) or value > 0:
                eng.wait_ge(s, value)

        def iterations(eng, body):
            body(0)
            with eng.Fori(1, BT - 1) as i:
                body(i)
            body(BT - 1)

        def first(i):
            return isinstance(i, int) and i == 0

        def last(i):
            return isinstance(i, int) and i == BT - 1

        def tr_use(i, c, kind, n):
            return i * TR_PER_ITER + (T0 + TR_ORDER[c, kind, n])

        def tr_bank(c, kind, n):
            return tr[(T0 + TR_ORDER[c, kind, n]) % 2]

        def rows(t):
            return (min(SHIFTS, SPT * (t + 1)) - SPT * t) * F

        def fields(k):
            return min(JB, F - JB * k)

        @block.sync
        def _(sp):
            def ahead_of_wait(*values):
                for v in values:
                    if not isinstance(v, int):
                        sp.lower_val(v)
                return values

            def load_ids(b):
                row, reads = ahead_of_wait(b * P, b * (16 * F))
                wait(sp, gathered, reads)
                sp.dma_start(ids_sb[:, :], ids[bass.ds(row, P), :]).then_inc(ids_loaded, 16)

            load_ids(0)
            w0v = W0.rearrange("h (a k) -> h a k", k=F)
            w0xv = w0x[:, 0:FX * F].rearrange("p (a k) -> p a k", k=FX)
            sp.dma_start(w0xv[:, :, 0:F], w0v).then_inc(w0_loaded, 16)
            sp.dma_start(w0xv[:, :, F:FX], w0v[:, :, 0:FX - F]).then_inc(w0_loaded, 16)
            sp.dma_start(w0y[:, 0:F * F], W0).then_inc(w0_loaded, 16)
            sp.dma_start(w0y[:, F * F:FX * F], W0[:, 0:(FX - F) * F]).then_inc(w0_loaded, 16)
            sp.dma_start(w1raw[:, 0:F * H], W1).then_inc(w1_loaded, 16)
            with nc.allow_non_contiguous_dma(reason="biases and the last layer's weights, once"):
                sp.dma_start(b0c[:, :], b0.rearrange("(p o) -> p o", o=1)).then_inc(small_loaded, 16)
                sp.dma_start(b1rep[:, :], b1.rearrange("(o h) -> o h", o=1).to_broadcast([P, H])).then_inc(small_loaded, 16)
                sp.dma_start(b2c[:, :], b2.rearrange("(p o) -> p o", o=1)).then_inc(small_loaded, 16)
                sp.dma_start(bt1[:, :], b_top1.rearrange("(m p) -> p m", p=P)).then_inc(small_loaded, 16)
                sp.dma_start(bt2[:, :], b_top2.rearrange("(m p) -> p m", p=P)).then_inc(small_loaded, 16)
                sp.dma_start(wt3[:, :], W_top3.rearrange("(m p) o -> p (m o)", p=P)).then_inc(small_loaded, 16)
            sp.dma_start(wt1[:, :, :], W_top1[0:3 * H, :].rearrange("(k p) n -> p k n", p=P)).then_inc(small_loaded, 16)
            sp.dma_start(wt1d[:, :], W_top1[3 * H:3 * H + ND, :]).then_inc(small_loaded, 16)
            sp.dma_start(wt2[:, :, :], W_top2.rearrange("(k p) n -> p k n", p=P)).then_inc(small_loaded, 16)

            sp.wait_ge(w0_summed, SHIFTS)
            sp.dma_start(w2raw[:, 0:F * H], W2).then_inc(w2_loaded, 16)

            x2_rows = x2_dram.rearrange("(b d) k -> b d k", d=D)

            def load_dense(k):
                sp.dma_start(dn[:, :], dense_ctx[bass.ds(k * P, P), :]).then_inc(dense_loaded, 16)

            def store_y(k):
                sp.dma_start(out[bass.ds(k * P, P), :].rearrange("b o -> o b"), y_sb[:, :]).then_inc(y_free, 16)

            def body(i):
                if not last(i):
                    load_ids(i + 1)
                if not first(i):
                    load_dense(i - 1)
                for u in range(D):
                    loads, tiles = ahead_of_wait(i * 32, i * D + u + 1)
                    if u == 0 and not first(i):
                        wait(sp, x2_loaded, loads)
                    wait(sp, x2_ready, tiles)
                    sp.dma_start(x2_rows[:, u, :], x2t[:, u % X2_SLOTS, :]).then_inc(x2_stored[u % X2_SLOTS], 16)
                stores, uses = ahead_of_wait((i + 1) * (16 * D // X2_SLOTS), i * GU)
                for n in range(X2_SLOTS):
                    wait(sp, x2_stored[n], stores)
                if not first(i):
                    wait(sp, tail_done, uses)
                for half in (slice(0, NG // 2), slice(NG // 2, NG)):
                    sp.dma_start(x2g[:, half, :], x2_dram.rearrange("(g r) k -> r g k", r=P)[:, half, :])\
                        .then_inc(x2_loaded, 16)
                if not first(i):
                    store_y(i - 1)

            iterations(sp, body)
            load_dense(BT - 1)
            sp.wait_ge(tail_done, BT * GU)
            store_y(BT - 1)
            sp.wait_ge(y_free, 16 * (BT + 1))

        @block.gpsimd
        def _(pool):
            pool.memset(y_sb[:, :], 0.0).then_inc(y_free, 16)
            pool.memset(ident[:, :], 0.0).then_inc(consts_done, 1)
            pool.memset(mask[:, :], 1.0).then_inc(consts_done, 1)
            pool.wait_ge(consts_done, 2)
            pool.affine_select(out=ident[:, :], in_=ident[:, :], compare_op=ALU.not_equal, fill=1.0,
                               base=0, pattern=[[-1, P]], channel_multiplier=1).then_inc(consts_done, 1)
            pool.affine_select(out=mask[:, :], in_=mask[:, :], compare_op=ALU.is_ge, fill=0.0,
                               base=0, pattern=[[-D, 8]], channel_multiplier=1).then_inc(consts_done, 1)
            pool.wait_ge(consts_done, 4)
            pool.affine_select(out=mask[:, :], in_=mask[:, :], compare_op=ALU.is_ge, fill=0.0,
                               base=D - 1, pattern=[[D, 8]], channel_multiplier=-1).then_inc(consts_done, 1)

            def gather(f):
                pool.indirect_dma_start(out=e_land[:, f, :], out_offset=None, in_=tables[f],
                                        in_offset=bass.IndirectOffsetOnAxis(ap=ids_sb[:, f:f + 1], axis=0),
                                        ).then_inc(gathered, 16)

            pool.wait_ge(ids_loaded, 16)
            for f in range(F):
                gather(f)

            def add_banks(i, u):
                for e in range(HALF - 1):
                    wait(pool, prods_ready, i * (D * HALF) + (u * HALF + e + 2))
                    wait(pool, prods_added, i * (D * (HALF - 1)) + (u * (HALF - 1) + e))
                    n = JB * H if e + 2 < HALF else fields(NB - 1) * H
                    left = prods[:, (u * HALF) % PROD_SLOTS, 0:n] if e == 0 else psum4[:, 0:n]
                    pool.tensor_tensor(psum4[:, 0:n], left, prods[:, (u * HALF + e + 1) % PROD_SLOTS, 0:n],
                                       ALU.add).then_inc(prods_added, 1)

            def finish_tile(i, u):
                wait(pool, prods_added, i * (D * (HALF - 1)) + ((u + 1) * (HALF - 1)))
                pool.tensor_tensor(psum2[:, :], psum4[:, 0:2 * H], psum4[:, 2 * H:4 * H], ALU.add).then_inc(folded, 1)
                wait(pool, folded, i * (2 * D) + (2 * u + 1))
                pool.tensor_tensor(psum1[:, :], psum2[:, 0:H], psum2[:, H:2 * H], ALU.add).then_inc(folded, 1)
                wait(pool, folded, i * (2 * D) + (2 * u + 2))
                wait(pool, ab_ready, i * D + (u + 1))
                wait(pool, x2_stored[u % X2_SLOTS], (i * (D // X2_SLOTS) + u // X2_SLOTS) * 16)
                pool.tensor_tensor(x2t[:, u % X2_SLOTS, :], psum1[:, :], ab[:, u % 2, :], ALU.add).then_inc(x2_ready, 1)

            def body(i):
                for u in range(D):
                    if u == 0 and not last(i):
                        wait(pool, ids_loaded, (i + 2) * 16)
                        wait(pool, e_copied, (i + 1) * 2)
                    add_banks(i, u)
                    if not last(i):
                        for f in range(4 * u, min(4 * u + 4, F)):
                            gather(f)
                    finish_tile(i, u)

            iterations(pool, body)

        @block.tensor
        def _(pe):
            pe.wait_ge(consts_done, 3)
            banks = yd + ya
            n = 0

            def transpose_weights(raw, cols, count):
                nonlocal n
                for g in range(0, count, 4):
                    if n >= 4:
                        if 2 <= n - 4 < 2 + NB:
                            pe.wait_ge(w_lo, n - 4 - 1)
                        else:
                            pe.wait_ge(w_hi, n - 3)
                    for t in range(g, min(g + 4, count)):
                        m = cols(t)
                        ins = pe.transpose(banks[n % 4][0:m.stop - m.start, (t - g) * P:(t - g + 1) * P],
                                           raw[:, m], ident[:, :])
                    ins.then_inc(wtr, 1)
                    n += 1

            pe.wait_ge(w0_summed, SHIFTS)
            transpose_weights(w0s, lambda t: slice(SPT * F * t, SPT * F * t + rows(t)), T0)
            pe.wait_ge(w1_loaded, 16)
            transpose_weights(w1raw, lambda t: slice(H * t, H * t + H), F)
            pe.wait_ge(w2_loaded, 16)
            transpose_weights(w2raw, lambda t: slice(H * t, H * t + H), F)

            def x0_transpose_waits(i, c):
                wait(pe, x1_out, (i * CH + c) * 2)
                wait(pe, e_copied, (i + (1 + c // CH)) * 2)

            def diag_transpose_waits(i, r):
                wait(pe, x0_out, i * (2 * CH) + (2 * CH - 1))
                wait(pe, tr_done, tr_use(i, 2, "diag", r) - 1)

            def x0_transpose(i, c):
                for d in range(DC):
                    ins = pe.transpose(l0[0:F, d * P:(d + 1) * P], e_tr[:, (c % CH) * DC + d, 0:F], ident[:, :])
                ins.then_inc(x0_tr, 1)

            def pair_transpose(i, c, t, use, bank):
                if t == 0:
                    wait(pe, pairs_made, (i * CH + c + 1) * DC)
                wait(pe, tr_done, use - 1)
                r = rows(t)
                for d in range(DC):
                    ins = pe.transpose(bank[0:r, d * P:(d + 1) * P],
                                       pairsT[:, d, SPT * F * t:SPT * F * t + r], ident[:, :])
                ins.then_inc(tr_ready, 1)

            def layer0(i, c, t, use):
                q = i * CH + c
                if t == 0:
                    wait(pe, x0_out, q * 2 + 1)
                wait(pe, tr_done, use + 1)
                slot = (c * T0 + t) % P_SLOTS
                pe.matmul(l0[:, :], lhsT=w0T[0:rows(t), t, :], rhs=pairs[0:rows(t), slot, :],
                          start=(t == 0), stop=(t == T0 - 1)).then_inc(l0_mm, 1)

            def diag_transpose(i, r):
                bank = tr_bank(2, "diag", r)
                for g in range(4):
                    rows_bd = x0bd[:, (4 * r + g) * 8:(4 * r + g + 1) * 8, :].rearrange("p b d -> p (b d)")
                    ins = pe.transpose(bank[:, g * F:(g + 1) * F], rows_bd, ident[0:F, 0:F])
                ins.then_inc(tr_ready, 1)

            def layer1_bank(i, c, s):
                dd, k = divmod(s, NB)
                u = c * DC + dd
                if s == 0:
                    wait(pe, x1_split, (i * CH + c) * 2 + 1)
                g = u * HALF + k // 2
                cols = slice(k * JB * H, (k * JB + fields(k)) * H)
                n = fields(k) * H
                if k % 2 == 0:
                    wait(pe, macs, i * (D * MACS) + (g - 1) * JB)
                    bank, ready = yd[g % 2], yd_ready
                else:
                    wait(pe, prods_ready, i * (D * HALF) + (g - 1))
                    bank, ready = ya[g % 2], ya_ready
                hi = x1hi[:, c, dd * P:(dd + 1) * P]
                lo = x1lo[:, c, dd * P:(dd + 1) * P]
                pe.matmul(bank[:, 0:n], lhsT=hi, rhs=w1hi[:, cols], start=True, stop=False)
                pe.matmul(bank[:, 0:n], lhsT=hi, rhs=w1lo[:, cols], start=False, stop=False)
                pe.matmul(bank[:, 0:n], lhsT=lo, rhs=w1hi[:, cols], start=False, stop=True).then_inc(ready, 1)

            def group(k, g):
                if g == 0:
                    wait(pe, x2_loaded, (k + 1) * 32)
                    wait(pe, tr_done, tr_use(k, 2, "diag", 3) + 1)
                    wait(pe, setup_done, 1)
                else:
                    wait(pe, tail_done, k * GU + g)
                pe.matmul(tail[:, 0:8 * JX], lhsT=x2g[:, g, :],
                          rhs=diag[:, g, :, :].rearrange("p b j -> p (b j)"),
                          start=True, stop=True).then_inc(tail_ready, 1)

            def dense_transpose(k):
                wait(pe, dense_loaded, (k + 1) * 16)
                wait(pe, tail_done, k * GU + NG)
                pe.transpose(tail[0:ND, 0:P], dn[:, :], ident[:, :]).then_inc(tail_ready, 1)

            def layer2(k, n):
                if n == 0:
                    wait(pe, tail_done, k * GU + NG + 1)
                for j in range(3 * n, 3 * n + 3):
                    ins = pe.matmul(tail[:, 0:P], lhsT=w2T[:, j, :], rhs=gram[:, j, :],
                                    start=(j == 0), stop=(j == F - 1))
                if n == F // 3 - 1:
                    ins.then_inc(tail_ready, 1)

            def top1(k):
                wait(pe, z0_done, k + 1)
                wait(pe, tail_done, k * GU + NG + 2)
                for m in range(TOP1 // P):
                    cols = slice(m * P, (m + 1) * P)
                    pe.matmul(tail[:, cols], lhsT=wt1[:, 0, cols], rhs=z0T[:, :], start=True, stop=False)
                    pe.matmul(tail[:, cols], lhsT=wt1[:, 1, cols], rhs=gram[:, F, :], start=False, stop=False)
                    pe.matmul(tail[:, cols], lhsT=wt1[:, 2, cols], rhs=z2T[:, :], start=False, stop=False)
                    ins = pe.matmul(tail[:, cols], lhsT=wt1d[:, cols], rhs=dnT[:, :], start=False, stop=True)
                ins.then_inc(tail_ready, 1)

            def top2(k):
                wait(pe, tail_done, k * GU + NG + 3)
                for m in range(TOP2 // P):
                    cols = slice(m * P, (m + 1) * P)
                    for t in range(TOP1 // P):
                        ins = pe.matmul(tail[:, cols], lhsT=wt2[:, t, cols], rhs=h1T[:, t, :],
                                        start=(t == 0), stop=(t == TOP1 // P - 1))
                ins.then_inc(tail_ready, 1)

            def top3(k):
                wait(pe, tail_done, k * GU + NG + 4)
                for t in range(TOP2 // P):
                    ins = pe.matmul(tail[0:1, 0:P], lhsT=wt3[:, t:t + 1], rhs=h2T[:, t, :],
                                    start=(t == 0), stop=(t == TOP2 // P - 1))
                ins.then_inc(tail_ready, 1)

            def tail_steps(k, c, s):
                if (c, s) in G_AT:
                    group(k, G_AT[c, s])
                if (c, s) == DENSE_AT:
                    dense_transpose(k)
                if (c, s) in W2_AT:
                    layer2(k, W2_AT[c, s])
                if (c, s) == TOP1_AT:
                    top1(k)
                if (c, s) == TOP2_AT:
                    top2(k)
                if (c, s) == TOP3_AT:
                    top3(k)

            pe.wait_ge(w_hi, 2)
            x0_transpose_waits(0, 0)
            x0_transpose(0, 0)
            pair_transpose(0, 0, 0, 0, tr[0])
            for t in range(T0):
                if t + 1 < T0:
                    pair_transpose(0, 0, t + 1, t + 1, tr[(t + 1) % 2])
                layer0(0, 0, t, t)
            pe.wait_ge(w_hi, n)
            pe.wait_ge(w_lo, NB)
            pe.wait_ge(small_loaded, 16 * 9)

            def body(i):
                for c in range(CH):
                    ahead = not (last(i) and c == CH - 1)
                    for s in range(SLOTS):
                        if ahead and s == S_A:
                            x0_transpose_waits(i, c + 1)
                        t, off = divmod(s - S_B, EVERY)
                        if ahead and off == 0 and 0 <= t < T0:
                            pair_transpose(i, c + 1, t, tr_use(i, c, "pair", t), tr_bank(c, "pair", t))
                        t, off = divmod(s - S_MM, EVERY)
                        if ahead and off == 0 and 0 <= t < T0:
                            layer0(i, c + 1, t, tr_use(i, c, "pair", t))
                        if (c, s) in DIAG_AT:
                            diag_transpose_waits(i, DIAG_AT[c, s])
                        if not first(i):
                            tail_steps(i - 1, c, s)
                        layer1_bank(i, c, s)
                        if ahead and s == S_A:
                            x0_transpose(i, c + 1)
                        if (c, s) in DIAG_AT:
                            diag_transpose(i, DIAG_AT[c, s])

            iterations(pe, body)
            for c in range(CH):
                for s in range(SLOTS):
                    tail_steps(BT - 1, c, s)

        @block.scalar
        def _(act):
            banks = yd + ya
            act.wait_ge(wtr, 1)
            act.activation(w0T[:, 0:4, :], banks[0][0:SPT * F, :].rearrange("p (t h) -> p t h", h=H),
                           ACT.Copy).then_inc(w_hi, 1)
            act.wait_ge(wtr, 2)
            short = T0 - 1
            act.activation(w0T[:, 4:short, :], banks[1][0:SPT * F, 0:(short - 4) * P].rearrange("p (t h) -> p t h", h=H),
                           ACT.Copy)
            act.activation(w0T[0:rows(short), short, :], banks[1][0:rows(short), (short - 4) * P:(T0 - 4) * P],
                           ACT.Copy).then_inc(w_hi, 1)

            def copy_fields(b):
                act.wait_ge(gathered, (b + 1) * (16 * F))
                view = e_land[:, :, :].rearrange("p f d -> p d f")
                act.activation(e_tr[:, :, 0:F], view, ACT.Copy).then_inc(e_copied, 1)
                act.activation(e_tr[:, :, F:FX], view[:, :, 0:FX - F], ACT.Copy).then_inc(e_copied, 1)

            def weights():
                n = 2
                for g in range(NB):
                    m = fields(g) * H
                    act.wait_ge(wtr, n + 1)
                    act.activation(w1hi[:, g * JB * H:g * JB * H + m], banks[n % 4][:, 0:m], ACT.Copy).then_inc(w_hi, 1)
                    n += 1
                for g in range(NB):
                    act.wait_ge(wtr, n + 1)
                    act.activation(w2T[:, g * JB:g * JB + fields(g), :],
                                   banks[n % 4][:, 0:fields(g) * H].rearrange("p (t h) -> p t h", h=H), ACT.Copy)\
                        .then_inc(w_hi, 1)
                    n += 1
                act.wait_ge(small_loaded, 16 * 9)
                act.activation(b2sum[:, :], b2c[:, :], ACT.Copy, scale=float(D)).then_inc(w_hi, 1)

            def x0_copies(i, c):
                q = i * CH + c
                cc = c % CH
                wait(act, x0_tr, q + 1)
                if cc == 0 and c == CH:
                    wait(act, tr_ready, tr_use(i, 2, "diag", 3) + 1)
                act.activation(x0bd[:, :, cc * DC:(cc + 1) * DC].rearrange("p b d -> p d b"),
                               l0[0:F, :].rearrange("p (d b) -> p d b", b=P), ACT.Copy).then_inc(x0_out, 1)
                wait(act, macs, (i * CH + c - CH + 1) * (DC * MACS) if not first(i) or c >= CH else 0)
                act.activation(e_sc[:, cc * DC:(cc + 1) * DC, :], e_tr[:, cc * DC:(cc + 1) * DC, 0:F],
                               ACT.Copy).then_inc(x0_out, 1)

            def pair_copy(i, c, t, use, bank):
                wait(act, tr_ready, use + 1)
                wait(act, l0_mm, (i * CH + c) * T0 + (t - P_SLOTS + 1))
                act.activation(pairs[0:rows(t), (c * T0 + t) % P_SLOTS, :], bank[0:rows(t), :], ACT.Copy)\
                    .then_inc(tr_done, 1)

            def diag_blocks(i, r):
                wait(act, tr_ready, tr_use(i, 2, "diag", r) + 1)
                if r == 0:
                    if first(i):
                        wait(act, setup_done, 1)
                    else:
                        wait(act, tail_ready, (i - 1) * GU + NG)
                x0 = tr_bank(2, "diag", r)[:, 0:4 * F].rearrange("p (g j) -> p g j", j=F)
                for b in range(8):
                    ins = act.activation(diag[:, 4 * r:4 * r + 4, b, 0:F], x0, ACT.Copy, scale=mask[:, b:b + 1])
                ins.then_inc(tr_done, 1)

            def x1_copies(i, c):
                q = i * CH + c
                wait(act, l0_mm, (q + 1) * T0)
                wait(act, x1_split, (q - 1) * 2)
                act.activation(x1f[:, c % 2, :], l0[:, :], ACT.Identity, bias=b0c[:, :]).then_inc(x1_out, 1)
                wait(act, ya_ready, (q - CH + 1) * (DC * HALF))
                act.activation(x1hi[:, c % CH, :], l0[:, :], ACT.Identity, bias=b0c[:, :]).then_inc(x1_out, 1)

            def layer1_bank(i, c, s):
                dd, k = divmod(s, NB)
                u = c * DC + dd
                g = u * HALF + k // 2
                if s < NB and k == 1:
                    wait(act, x0_out, (i * CH + c + 1) * 2)
                wait(act, ya_ready, i * (D * HALF) + g + 1)
                before = g - PROD_SLOTS
                uu, kk = divmod(before, HALF)
                wait(act, prods_added, i * (D * (HALF - 1)) + (uu * (HALF - 1) + max(kk, 1)))
                for j in range(fields(k)):
                    ins = act.activation(prods[:, g % PROD_SLOTS, j * H:(j + 1) * H], ya[g % 2][:, j * H:(j + 1) * H],
                                         ACT.Copy, scale=e_sc[:, u, k * JB + j:k * JB + j + 1])
                ins.then_inc(prods_ready, 1)

            def tail_steps(k, c, s):
                if (c, s - 1) in G_AT:
                    g = G_AT[c, s - 1]
                    wait(act, tail_ready, k * GU + g + 1)
                    act.activation(gram[:, :, 8 * g:8 * g + 8],
                                   tail[:, 0:8 * JX].rearrange("p (b j) -> p j b", j=JX), ACT.Copy).then_inc(tail_done, 1)
                if (c, s - 1) == DENSE_AT:
                    wait(act, tail_ready, k * GU + NG + 1)
                    act.activation(dnT[:, :], tail[0:ND, 0:P], ACT.Copy).then_inc(tail_done, 1)
                if (c, s - 2) == (2, 36):
                    wait(act, tail_ready, k * GU + NG + 2)
                    act.activation(z2T[:, :], tail[:, 0:P], ACT.Identity, bias=b2sum[:, :]).then_inc(tail_done, 1)
                if (c, s - 2) == TOP1_AT:
                    wait(act, tail_ready, k * GU + NG + 3)
                    for m in range(TOP1 // P):
                        ins = act.activation(h1T[:, m, :], tail[:, m * P:(m + 1) * P], ACT.Relu, bias=bt1[:, m:m + 1])
                    ins.then_inc(tail_done, 1)
                if (c, s - 1) == TOP2_AT:
                    wait(act, tail_ready, k * GU + NG + 4)
                    for m in range(TOP2 // P):
                        ins = act.activation(h2T[:, m, :], tail[:, m * P:(m + 1) * P], ACT.Relu, bias=bt2[:, m:m + 1])
                    ins.then_inc(tail_done, 1)
                if (c, s - 1) == TOP3_AT:
                    wait(act, tail_ready, k * GU + NG + 5)
                    wait(act, y_free, (k + 1) * 16)
                    act.activation(y_sb[:, :], tail[0:1, 0:P], ACT.Copy).then_inc(tail_done, 1)

            weights()
            copy_fields(0)
            x0_copies(0, 0)
            for t in range(T0):
                pair_copy(0, 0, t, t, tr[t % 2])
            x1_copies(0, 0)

            def body(i):
                for c in range(CH):
                    ahead = not (last(i) and c == CH - 1)
                    for s in range(SLOTS):
                        if ahead and s == S_A + 1:
                            x0_copies(i, c + 1)
                        if ahead and s == S_X1:
                            x1_copies(i, c + 1)
                        t, off = divmod(s - S_B - 1, EVERY)
                        if ahead and off == 0 and 0 <= t < T0:
                            pair_copy(i, c + 1, t, tr_use(i, c, "pair", t), tr_bank(c, "pair", t))
                        if (c, s - 1) in DIAG_AT:
                            diag_blocks(i, DIAG_AT[c, s - 1])
                        if c == 2 and s == S_FIELDS and not last(i):
                            wait(act, pairs_made, (i + 1) * (CH * DC))
                            wait(act, x0_tr, (i + 1) * CH)
                            wait(act, x0_out, (i + 1) * (CH * 2))
                            copy_fields(i + 1)
                        if not first(i):
                            tail_steps(i - 1, c, s)
                        if s % 2 == 1:
                            layer1_bank(i, c, s)

            iterations(act, body)
            for c in range(CH):
                for s in range(SLOTS):
                    tail_steps(BT - 1, c, s)

        @block.vector
        def _(dve):
            def pair_products(i, c, d, use):
                if d == 0:
                    wait(dve, e_copied, (i + (1 + c // CH)) * 2)
                    if use is not None:
                        wait(dve, tr_ready, use + 1)
                x0 = e_tr[:, (c % CH) * DC + d, :]
                one = x0[:, 0:F].rearrange("p (o a) -> p o a", o=1).to_broadcast([P, SHIFTS, F])
                other = bass.AP(tensor=x0.tensor, offset=x0.offset, ap=[x0.ap[0], [1, SHIFTS], [1, F]])
                dve.tensor_tensor(pairsT[:, d, :].rearrange("p (s a) -> p s a", a=F), one, other,
                                  ALU.mult).then_inc(pairs_made, 1)

            dve.wait_ge(w0_loaded, 16 * 4)
            diagonal = w0x[:, :].rearrange("p (a r) -> p r a", r=FX + 1)
            for s in range(SHIFTS):
                dst = w0s[:, s * F:(s + 1) * F]
                if s == 0:
                    dve.tensor_copy(dst, diagonal[:, 0, :]).then_inc(w0_summed, 1)
                else:
                    other = w0y[:, s * F:s * F + (F + 1) * F].rearrange("p (a r) -> p r a", r=F + 1)[:, 0, :]
                    dve.tensor_tensor(dst, diagonal[:, s, :], other, ALU.add).then_inc(w0_summed, 1)

            banks = yd + ya
            for g in range(NB):
                dve.wait_ge(w_hi, 2 + g + 1)
                cols = slice(g * JB * H, (g * JB + fields(g)) * H)
                dve.tensor_tensor(w1lo[:, cols], banks[(2 + g) % 4][:, 0:fields(g) * H],
                                  w1hi[:, cols].bitcast(F32), ALU.subtract).then_inc(w_lo, 1)
            dve.wait_ge(consts_done, 5)
            dve.wait_ge(wtr, 2 + 2 * NB)
            dve.tensor_copy(diag[:, :, :, F], mask[:, :].rearrange("p (o b) -> p o b", o=1).to_broadcast([P, NG, 8]))\
                .then_inc(setup_done, 1)

            def x1_remainder(i, c):
                q = i * CH + c
                wait(dve, x1_out, (q + 1) * 2)
                dve.tensor_tensor(x1lo[:, c % CH, :], x1f[:, c % 2, :], x1hi[:, c % CH, :].bitcast(F32),
                                  ALU.subtract).then_inc(x1_split, 1)
                wait(dve, z0_done, i + (c // CH))
                dve.tensor_reduce(z0part[:, c % CH, :], x1f[:, c % 2, :].rearrange("p (d b) -> p b d", b=P),
                                  AX.X, ALU.add).then_inc(x1_split, 1)

            def z0_total(i):
                if not first(i):
                    wait(dve, tail_ready, (i - 1) * GU + NG + 3)
                wait(dve, x1_split, (i + 1) * (2 * CH))
                dve.tensor_reduce(z0T[:, :], z0part[:, :, :].rearrange("p c b -> p b c"), AX.X, ALU.add)\
                    .then_inc(z0_done, 1)

            def layer1_bank(i, c, s):
                dd, k = divmod(s, NB)
                u = c * DC + dd
                g = u * HALF + k // 2
                if s == 0:
                    wait(dve, x0_out, (i * CH + c + 1) * 2)
                wait(dve, yd_ready, i * (D * HALF) + g + 1)
                if k == 0:
                    wait(dve, ab_ready, i * D + (u - 1))
                for j in range(JB):
                    m = (k // 2) * JB + j
                    a = acc[:, u % 2, m % 2, :]
                    y = yd[g % 2][:, j * H:(j + 1) * H]
                    x = e_sc[:, u, k * JB + j:k * JB + j + 1]
                    if m == 0:
                        ins = dve.scalar_tensor_tensor(a, y, x, b1rep[:, :], ALU.mult, ALU.add)
                    elif m == 1:
                        ins = dve.tensor_scalar(a, y, x, None, ALU.mult)
                    else:
                        wait(dve, macs, i * (D * MACS) + (u * MACS + m - 1))
                        ins = dve.scalar_tensor_tensor(a, y, x, a, ALU.mult, ALU.add)
                    ins.then_inc(macs, 1)
                if k == NB - 2:
                    wait(dve, macs, i * (D * MACS) + (u + 1) * MACS)
                    wait(dve, x2_ready, i * D + (u - 1))
                    dve.tensor_tensor(ab[:, u % 2, :], acc[:, u % 2, 0, :], acc[:, u % 2, 1, :], ALU.add)\
                        .then_inc(ab_ready, 1)

            dve.wait_ge(wtr, 2)
            for d in range(DC):
                pair_products(0, 0, d, None)
            for d in range(DC):
                pair_products(0, 1, d, T0 - 1)
            x1_remainder(0, 0)

            def body(i):
                for c in range(CH):
                    ahead = not (last(i) and c == CH - 1)
                    for s in range(SLOTS):
                        if s in S_PAIRS and not (last(i) and c >= 2):
                            pair_products(i, c + 2, S_PAIRS.index(s), tr_use(i, c, "pair", T0 - 1))
                        if (c, s) == (3, 14):
                            z0_total(i)
                        if ahead and s == S_XL:
                            x1_remainder(i, c + 1)
                        if s % 2 == 0:
                            layer1_bank(i, c, s)

            iterations(dve, body)


def kernel(**inputs):
    import numpy as _np
    import concourse.bacc as _bacc
    from concourse import mybir as _mybir
    from concourse.bass_utils import run_bass_kernel_spmd as _run

    nc = _bacc.Bacc("TRN2", target_bir_lowering=False, num_devices=1)
    arrays, aps = {}, {}
    for name, value in inputs.items():
        a = _np.ascontiguousarray(value)
        arrays[f"in_{name}"] = a
        aps[name] = nc.dram_tensor(f"in_{name}", a.shape, _mybir.dt.from_np(a.dtype), kind="ExternalInput").ap()
    out = nc.dram_tensor("out_y", (B, 1), F32, kind="ExternalOutput").ap()
    cin_tower(nc, aps["dense_ctx"], aps["ids"], [aps[f"tbl_{f}"] for f in range(F)],
              aps["W_top1"], aps["b_top1"], aps["W_top2"], aps["b_top2"], aps["W_top3"],
              aps["L0_rec_W0"], aps["L0_rec_b0"], aps["L0_rec_W1"], aps["L0_rec_b1"],
              aps["L0_rec_W2"], aps["L0_rec_b2"], out)
    r = _run(nc, [arrays], core_ids=[0])
    return r.results[0]["out_y"]
```

```python
import concourse.bass as bass
from concourse import mybir
from contextlib import ExitStack

F32 = mybir.dt.float32
F32R = mybir.dt.float32r
I32 = mybir.dt.int32
ALU = mybir.AluOpType
ACT = mybir.ActivationFunctionType
AX = mybir.AxisListType

P = 128
B = 1024
F = 39
D = 16
H = 128
BT = B // P
DC = 4
CH = D // DC
SHIFTS = (F + 1) // 2
SPT = 3
T0 = -(-SHIFTS // SPT)
FX = F + SHIFTS - 1
JB = 4
NB = -(-F // JB)
HALF = NB // 2
MACS = HALF * JB
PROD_SLOTS = 5
P_SLOTS = 2
X2_SLOTS = 2
NG = P // 8
JX = F + 1
GU = NG + 5
TOP1, TOP2, ND = 512, 256, 16
SLOTS = DC * NB

S_A, S_B, S_MM, S_X1, S_XL, EVERY = 0, 2, 6, 32, 34, 4
S_FIELDS = 22
S_PAIRS = {c: tuple(range(5, 5 + 4 * T0, 4)) if c != 2 else tuple(range(25, 25 + 2 * T0, 2)) for c in range(CH)}
G_AT = {((20 + 4 * g) // SLOTS, (20 + 4 * g) % SLOTS): g for g in range(NG)}
DENSE_AT = (2, 4)
W2_AT = {(2, 11 + 2 * n): n for n in range(13)}
TOP1_AT, TOP2_AT, TOP3_AT = (3, 3), (3, 13), (3, 18)
DIAG_AT = {(2, 4 + 7 * r): r for r in range(4)}
DIAG_PARTS = (1, 3)


GATHERS = 3
EARLY = 5
EARLY_FIELDS = GATHERS * EARLY


def transposed_bank_order():
    order = {}
    for c in range(CH):
        steps = [(S_B + EVERY * t, "pair", t) for t in range(T0)]
        steps += [(s, "diag", r) for (cc, s), r in DIAG_AT.items() if cc == c]
        for _, kind, n in sorted(steps):
            order[c, kind, n] = len(order)
    return order


TR_ORDER = transposed_bank_order()
TR_PER_ITER = len(TR_ORDER)


def cin_tower(nc, dense_ctx, ids, tables, W_top1, b_top1, W_top2, b_top2, W_top3,
              W0, b0, W1, b1, W2, b2, out):
    x2_dram = nc.dram_tensor("x2_scratch", (P * D, H), F32, kind="Internal").ap()
    ctx = ExitStack()
    with ctx:
        def sb(name, shape, dt=F32):
            return ctx.enter_context(nc.sbuf_tensor(name, shape, dt))

        def pb(name):
            return ctx.enter_context(nc.psum_tensor(name, [P, 512], F32))

        def sem(name):
            return ctx.enter_context(nc.semaphore(name))

        ident = sb("ident", [P, P])
        mask = sb("mask", [P, 8])
        ids_sb = sb("ids_sb", [P, F], I32)
        e_land = sb("e_land", [P, F, D])
        e_tr = sb("e_tr", [P, D, FX])
        e_sc = sb("e_sc", [P, D, F])
        pairsT = sb("pairsT", [P, DC, SHIFTS * F])
        x0bd = sb("x0bd", [F, P, D])
        pairs_hi = sb("pairs_hi", [SPT * F, P_SLOTS, 512], F32R)
        pairs_lo = sb("pairs_lo", [SPT * F, P_SLOTS, 512], F32R)
        w0s = pairsT[:, 0, :]
        w0hi = sb("w0hi", [SPT * F, T0, H], F32R)
        w0lo = sb("w0lo", [SPT * F, T0, H], F32R)
        x1f = sb("x1f", [P, 512])
        x1hi = sb("x1hi", [P, CH, 512], F32R)
        x1lo = sb("x1lo", [P, CH, 512], F32R)
        z0part = sb("z0part", [P, CH, P])
        w1hi = sb("w1hi", [P, F * H], F32R)
        w1lo = sb("w1lo", [P, F * H], F32R)
        w2T = sb("w2T", [P, F, H])
        prods = sb("prods", [P, PROD_SLOTS, JB * H])
        acc = sb("acc", [P, 2, 2, H])
        ab = sb("ab", [P, 2, H])
        psum4 = sb("psum4", [P, JB * H])
        psum2 = sb("psum2", [P, 2 * H])
        psum1 = sb("psum1", [P, H])
        x2t = sb("x2t", [P, X2_SLOTS, H])
        x2g = sb("x2g", [P, NG, H])
        diag = sb("diag", [P, NG, 8, JX])
        gram = sb("gram", [P, JX, P])
        w1raw = gram[:, :, :].rearrange("p j b -> p (j b)")
        w2raw = diag[:, :, :, :].rearrange("p g b j -> p (g b j)")
        W0N = (FX + 1) * F
        w0x = w2raw[:, 0:W0N]
        w0y = w2raw[:, W0N:2 * W0N]
        b0c = sb("b0c", [P, 1])
        b1rep = sb("b1rep", [P, H])
        b2c = sb("b2c", [P, 1])
        b2sum = sb("b2sum", [P, 1])
        bt1 = sb("bt1", [P, TOP1 // P])
        bt2 = sb("bt2", [P, TOP2 // P])
        wt1 = sb("wt1", [P, 3, TOP1])
        wt1d = sb("wt1d", [ND, TOP1])
        wt2 = sb("wt2", [P, TOP1 // P, TOP2])
        wt3 = sb("wt3", [P, TOP2 // P])
        z0T = sb("z0T", [P, P])
        z2T = sb("z2T", [P, P])
        dn = sb("dn", [P, ND])
        dnT = sb("dnT", [ND, P])
        h1T = sb("h1T", [P, TOP1 // P, P])
        h2T = sb("h2T", [P, TOP2 // P, P])
        y_sb = sb("y_sb", [1, P])

        yd = [pb("yd0"), pb("yd1")]
        ya = [pb("ya0"), pb("ya1")]
        tr = [pb("tr0"), pb("tr1")]
        l0 = pb("l0")
        tail = pb("tail")

        consts_done = sem("consts_done")
        w0_loaded = sem("w0_loaded")
        w1_loaded = sem("w1_loaded")
        w2_loaded = sem("w2_loaded")
        small_loaded = sem("small_loaded")
        w0_summed = sem("w0_summed")
        wtr = sem("wtr")
        w_hi = sem("w_hi")
        w_lo = sem("w_lo")
        setup_done = sem("setup_done")
        ids_loaded = sem("ids_loaded")
        gathered = sem("gathered")
        e_copied = sem("e_copied")
        x0_tr = sem("x0_tr")
        x0_out = sem("x0_out")
        pairs_made = sem("pairs_made")
        tr_ready = sem("tr_ready")
        pairs_rounded = sem("pairs_rounded")
        pairs_split = sem("pairs_split")
        diag_made = sem("diag_made")
        l0_mm = sem("l0_mm")
        x1_out = sem("x1_out")
        x1_split = sem("x1_split")
        z0_done = sem("z0_done")
        yd_ready = sem("yd_ready")
        ya_ready = sem("ya_ready")
        macs = sem("macs")
        ab_ready = sem("ab_ready")
        prods_ready = sem("prods_ready")
        prods_added = sem("prods_added")
        folded = sem("folded")
        x2_ready = sem("x2_ready")
        x2_stored = [sem(f"x2_stored{n}") for n in range(X2_SLOTS)]
        x2_loaded = [sem("x2_loaded0"), sem("x2_loaded1")]
        dense_loaded = sem("dense_loaded")
        tail_ready = sem("tail_ready")
        tail_done = sem("tail_done")
        y_free = sem("y_free")

        idle_banks = (tail, tr[0], tr[1], l0)

        block = ctx.enter_context(nc.Block())

        def wait(eng, s, value):
            if not isinstance(value, int) or value > 0:
                eng.wait_ge(s, value)

        def iterations(eng, body, ends=1):
            body(0)
            with eng.Fori(1, BT - ends) as i:
                body(i)
            for i in range(BT - ends, BT):
                body(i)

        def first(i):
            return isinstance(i, int) and i == 0

        def last(i):
            return isinstance(i, int) and i == BT - 1

        def more(i, n):
            return not isinstance(i, int) or i + n < BT

        def tr_use(i, c, kind, n):
            return i * TR_PER_ITER + (T0 + TR_ORDER[c, kind, n])

        def tr_bank(c, kind, n):
            return tr[(T0 + TR_ORDER[c, kind, n]) % 2]

        def rows(t):
            return (min(SHIFTS, SPT * (t + 1)) - SPT * t) * F

        def fields(k):
            return min(JB, F - JB * k)

        @block.sync
        def _(sp):
            def ahead_of_wait(*values):
                for v in values:
                    if not isinstance(v, int):
                        sp.lower_val(v)
                return values

            def load_ids(b):
                row, reads = ahead_of_wait(b * P, b * (16 * F))
                wait(sp, gathered, reads)
                sp.dma_start(ids_sb[:, :], ids[bass.ds(row, P), :]).then_inc(ids_loaded, 16)

            load_ids(0)
            w0v = W0.rearrange("h (a k) -> h a k", k=F)
            w0xv = w0x[:, 0:FX * F].rearrange("p (a k) -> p a k", k=FX)
            sp.dma_start(w0xv[:, :, 0:F], w0v).then_inc(w0_loaded, 16)
            sp.dma_start(w0xv[:, :, F:FX], w0v[:, :, 0:FX - F]).then_inc(w0_loaded, 16)
            sp.dma_start(w0y[:, 0:F * F], W0).then_inc(w0_loaded, 16)
            sp.dma_start(w0y[:, F * F:FX * F], W0[:, 0:(FX - F) * F]).then_inc(w0_loaded, 16)
            sp.dma_start(w1raw[:, 0:F * H], W1).then_inc(w1_loaded, 16)
            with nc.allow_non_contiguous_dma(reason="biases and the last layer's weights, once"):
                sp.dma_start(b0c[:, :], b0.rearrange("(p o) -> p o", o=1)).then_inc(small_loaded, 16)
                sp.dma_start(b1rep[:, :], b1.rearrange("(o h) -> o h", o=1).to_broadcast([P, H])).then_inc(small_loaded, 16)
                sp.dma_start(b2c[:, :], b2.rearrange("(p o) -> p o", o=1)).then_inc(small_loaded, 16)
                sp.dma_start(bt1[:, :], b_top1.rearrange("(m p) -> p m", p=P)).then_inc(small_loaded, 16)
                sp.dma_start(bt2[:, :], b_top2.rearrange("(m p) -> p m", p=P)).then_inc(small_loaded, 16)
                sp.dma_start(wt3[:, :], W_top3.rearrange("(m p) o -> p (m o)", p=P)).then_inc(small_loaded, 16)
            sp.dma_start(wt1[:, :, :], W_top1[0:3 * H, :].rearrange("(k p) n -> p k n", p=P)).then_inc(small_loaded, 16)
            sp.dma_start(wt1d[:, :], W_top1[3 * H:3 * H + ND, :]).then_inc(small_loaded, 16)
            sp.dma_start(wt2[:, :, :], W_top2.rearrange("(k p) n -> p k n", p=P)).then_inc(small_loaded, 16)

            sp.wait_ge(w0_summed, SHIFTS)
            sp.dma_start(w2raw[:, 0:F * H], W2).then_inc(w2_loaded, 16)

            x2_rows = x2_dram.rearrange("(b d) k -> b d k", d=D)

            def load_dense(k):
                sp.dma_start(dn[:, :], dense_ctx[bass.ds(k * P, P), :]).then_inc(dense_loaded, 16)

            def store_y(k):
                sp.dma_start(out[bass.ds(k * P, P), :].rearrange("b o -> o b"), y_sb[:, :]).then_inc(y_free, 16)

            load_ids(1)

            def body(i):
                if not first(i):
                    load_dense(i - 1)
                for u in range(D):
                    if u == D - EARLY - 1 and more(i, 2):
                        load_ids(i + 2)
                    loads, tiles = ahead_of_wait(i * 16, i * D + u + 1)
                    if u == 0 and not first(i):
                        wait(sp, x2_loaded[0], loads)
                        wait(sp, x2_loaded[1], loads)
                    wait(sp, x2_ready, tiles)
                    sp.dma_start(x2_rows[:, u, :], x2t[:, u % X2_SLOTS, :]).then_inc(x2_stored[u % X2_SLOTS], 16)
                stores, uses = ahead_of_wait((i + 1) * (16 * D // X2_SLOTS), i * GU)
                for n in range(X2_SLOTS):
                    wait(sp, x2_stored[n], stores)
                if not first(i):
                    wait(sp, tail_done, uses)
                for n in range(2):
                    half = slice(n * NG // 2, (n + 1) * NG // 2)
                    sp.dma_start(x2g[:, half, :], x2_dram.rearrange("(g r) k -> r g k", r=P)[:, half, :])\
                        .then_inc(x2_loaded[n], 16)
                if not first(i):
                    store_y(i - 1)

            iterations(sp, body, ends=2)
            load_dense(BT - 1)
            sp.wait_ge(tail_done, BT * GU)
            store_y(BT - 1)
            sp.wait_ge(y_free, 16 * (BT + 1))

        @block.gpsimd
        def _(pool):
            pool.memset(y_sb[:, :], 0.0).then_inc(y_free, 16)
            pool.memset(ident[:, :], 0.0).then_inc(consts_done, 1)
            pool.memset(mask[:, :], 1.0).then_inc(consts_done, 1)
            pool.wait_ge(consts_done, 2)
            pool.affine_select(out=ident[:, :], in_=ident[:, :], compare_op=ALU.not_equal, fill=1.0,
                               base=0, pattern=[[-1, P]], channel_multiplier=1).then_inc(consts_done, 1)
            pool.affine_select(out=mask[:, :], in_=mask[:, :], compare_op=ALU.is_ge, fill=0.0,
                               base=0, pattern=[[-D, 8]], channel_multiplier=1).then_inc(consts_done, 1)
            pool.wait_ge(consts_done, 4)
            pool.affine_select(out=mask[:, :], in_=mask[:, :], compare_op=ALU.is_ge, fill=0.0,
                               base=D - 1, pattern=[[D, 8]], channel_multiplier=-1).then_inc(consts_done, 1)

            def gather(f):
                pool.indirect_dma_start(out=e_land[:, f, :], out_offset=None, in_=tables[f],
                                        in_offset=bass.IndirectOffsetOnAxis(ap=ids_sb[:, f:f + 1], axis=0),
                                        ).then_inc(gathered, 16)

            pool.wait_ge(ids_loaded, 16)
            for f in range(F):
                gather(f)
            pool.wait_ge(ids_loaded, 32)
            pool.wait_ge(e_copied, 2)
            for f in range(EARLY_FIELDS):
                gather(f)

            def add_banks(i, u):
                for e in range(HALF - 1):
                    wait(pool, prods_ready, i * (D * HALF) + (u * HALF + e + 2))
                    wait(pool, prods_added, i * (D * (HALF - 1)) + (u * (HALF - 1) + e))
                    n = JB * H if e + 2 < HALF else fields(NB - 1) * H
                    left = prods[:, (u * HALF) % PROD_SLOTS, 0:n] if e == 0 else psum4[:, 0:n]
                    pool.tensor_tensor(psum4[:, 0:n], left, prods[:, (u * HALF + e + 1) % PROD_SLOTS, 0:n],
                                       ALU.add).then_inc(prods_added, 1)

            def finish_tile(i, u):
                wait(pool, prods_added, i * (D * (HALF - 1)) + ((u + 1) * (HALF - 1)))
                pool.tensor_tensor(psum2[:, :], psum4[:, 0:2 * H], psum4[:, 2 * H:4 * H], ALU.add).then_inc(folded, 1)
                wait(pool, folded, i * (2 * D) + (2 * u + 1))
                pool.tensor_tensor(psum1[:, :], psum2[:, 0:H], psum2[:, H:2 * H], ALU.add).then_inc(folded, 1)
                wait(pool, folded, i * (2 * D) + (2 * u + 2))
                wait(pool, ab_ready, i * D + (u + 1))
                wait(pool, x2_stored[u % X2_SLOTS], (i * (D // X2_SLOTS) + u // X2_SLOTS) * 16)
                pool.tensor_tensor(x2t[:, u % X2_SLOTS, :], psum1[:, :], ab[:, u % 2, :], ALU.add).then_inc(x2_ready, 1)

            def body(i):
                for u in range(D):
                    if u == D - EARLY and more(i, 2):
                        wait(pool, ids_loaded, (i + 3) * 16)
                        wait(pool, e_copied, (i + 2) * 2)
                    add_banks(i, u)
                    if u >= D - EARLY and more(i, 2):
                        for n in range(GATHERS):
                            gather((u - D + EARLY) * GATHERS + n)
                    if more(i, 1):
                        for f in range(EARLY_FIELDS + u * GATHERS, min(EARLY_FIELDS + (u + 1) * GATHERS, F)):
                            gather(f)
                    finish_tile(i, u)

            iterations(pool, body, ends=2)

        @block.tensor
        def _(pe):
            pe.wait_ge(consts_done, 3)
            banks = yd + ya
            n = 0

            def transpose_weights(raw, cols, count):
                nonlocal n
                for g in range(0, count, 4):
                    if n >= 4:
                        if n - 4 < 2 + NB:
                            pe.wait_ge(w_lo, n - 3)
                        else:
                            pe.wait_ge(w_hi, n - 3)
                    for t in range(g, min(g + 4, count)):
                        m = cols(t)
                        ins = pe.transpose(banks[n % 4][0:m.stop - m.start, (t - g) * P:(t - g + 1) * P],
                                           raw[:, m], ident[:, :])
                    ins.then_inc(wtr, 1)
                    n += 1

            pe.wait_ge(w0_summed, SHIFTS)
            transpose_weights(w0s, lambda t: slice(SPT * F * t, SPT * F * t + rows(t)), T0)
            pe.wait_ge(w1_loaded, 16)
            transpose_weights(w1raw, lambda t: slice(H * t, H * t + H), F)
            pe.wait_ge(w2_loaded, 16)
            transpose_weights(w2raw, lambda t: slice(H * t, H * t + H), F)

            def x0_transpose_waits(i, c):
                wait(pe, x1_out, (i * CH + c) * 2)
                wait(pe, e_copied, (i + (1 + c // CH)) * 2)

            def wait_tr_free(i, c, kind, n):
                before = TR_ORDER[c, kind, n] - 2
                if before < 0:
                    wait(pe, pairs_split, i * (CH * T0) + (T0 + before + 1))
                    return
                cc, kk, nn = next(key for key, use in TR_ORDER.items() if use == before)
                if kk == "pair":
                    wait(pe, pairs_split, i * (CH * T0) + ((cc + 1) * T0 + nn + 1))
                else:
                    wait(pe, diag_made, i * 4 + nn + 1)

            def diag_transpose_waits(i, r):
                wait(pe, x0_out, i * (2 * CH) + (2 * CH - 1))
                wait_tr_free(i, 2, "diag", r)

            def x0_transpose(i, c):
                for d in range(DC):
                    ins = pe.transpose(l0[0:F, d * P:(d + 1) * P], e_tr[:, (c % CH) * DC + d, 0:F], ident[:, :])
                ins.then_inc(x0_tr, 1)

            def pair_transpose(i, c, t, bank):
                wait(pe, pairs_made, (i * CH + c) * T0 + (t + 1))
                if c == 0:
                    wait(pe, pairs_split, t - 1)
                else:
                    wait_tr_free(i, c - 1, "pair", t)
                r = rows(t)
                for d in range(DC):
                    ins = pe.transpose(bank[0:r, d * P:(d + 1) * P],
                                       pairsT[:, d, SPT * F * t:SPT * F * t + r], ident[:, :])
                ins.then_inc(tr_ready, 1)

            def layer0(i, c, t):
                q = i * CH + c
                if t == 0:
                    wait(pe, x0_out, q * 2 + 1)
                wait(pe, pairs_split, q * T0 + (t + 1))
                slot = (c * T0 + t) % P_SLOTS
                hi, lo = pairs_hi[0:rows(t), slot, :], pairs_lo[0:rows(t), slot, :]
                whi, wlo = w0hi[0:rows(t), t, :], w0lo[0:rows(t), t, :]
                pe.matmul(l0[:, :], lhsT=whi, rhs=hi, start=(t == 0), stop=False)
                pe.matmul(l0[:, :], lhsT=wlo, rhs=hi, start=False, stop=False)
                pe.matmul(l0[:, :], lhsT=whi, rhs=lo, start=False, stop=(t == T0 - 1)).then_inc(l0_mm, 1)

            def diag_transpose(i, r):
                bank = tr_bank(2, "diag", r)
                for g in range(4):
                    rows_bd = x0bd[:, (4 * r + g) * 8:(4 * r + g + 1) * 8, :].rearrange("p b d -> p (b d)")
                    ins = pe.transpose(bank[:, g * F:(g + 1) * F], rows_bd, ident[0:F, 0:F])
                ins.then_inc(tr_ready, 1)

            def layer1_bank(i, c, s):
                dd, k = divmod(s, NB)
                u = c * DC + dd
                if s == 0:
                    wait(pe, x1_split, (i * CH + c) * 2 + 1)
                g = u * HALF + k // 2
                cols = slice(k * JB * H, (k * JB + fields(k)) * H)
                n = fields(k) * H
                if k % 2 == 0:
                    wait(pe, macs, i * (D * MACS) + (g - 1) * JB)
                    bank, ready = yd[g % 2], yd_ready
                else:
                    wait(pe, prods_ready, i * (D * HALF) + (g - 1))
                    bank, ready = ya[g % 2], ya_ready
                hi = x1hi[:, c, dd * P:(dd + 1) * P]
                lo = x1lo[:, c, dd * P:(dd + 1) * P]
                pe.matmul(bank[:, 0:n], lhsT=hi, rhs=w1hi[:, cols], start=True, stop=False)
                pe.matmul(bank[:, 0:n], lhsT=hi, rhs=w1lo[:, cols], start=False, stop=False)
                pe.matmul(bank[:, 0:n], lhsT=lo, rhs=w1hi[:, cols], start=False, stop=True).then_inc(ready, 1)

            def group(k, g, banks=(tail,)):
                if g % (NG // 2) == 0:
                    wait(pe, x2_loaded[2 * g // NG], (k + 1) * 16)
                if g == 0:
                    wait(pe, diag_made, (k + 1) * 4)
                    wait(pe, setup_done, 1)
                if g >= len(banks):
                    wait(pe, tail_done, k * GU + (g - len(banks) + 1))
                pe.matmul(banks[g % len(banks)][:, 0:8 * JX], lhsT=x2g[:, g, :],
                          rhs=diag[:, g, :, :].rearrange("p b j -> p (b j)"),
                          start=True, stop=True).then_inc(tail_ready, 1)

            def dense_transpose(k):
                wait(pe, dense_loaded, (k + 1) * 16)
                wait(pe, tail_done, k * GU + NG)
                pe.transpose(tail[0:ND, 0:P], dn[:, :], ident[:, :]).then_inc(tail_ready, 1)

            def layer2(k, n):
                if n == 0:
                    wait(pe, tail_done, k * GU + NG + 1)
                for j in range(3 * n, 3 * n + 3):
                    ins = pe.matmul(tail[:, 0:P], lhsT=w2T[:, j, :], rhs=gram[:, j, :],
                                    start=(j == 0), stop=(j == F - 1))
                if n == F // 3 - 1:
                    ins.then_inc(tail_ready, 1)

            def top1(k):
                wait(pe, z0_done, k + 1)
                wait(pe, tail_done, k * GU + NG + 2)
                for m in range(TOP1 // P):
                    cols = slice(m * P, (m + 1) * P)
                    pe.matmul(tail[:, cols], lhsT=wt1[:, 0, cols], rhs=z0T[:, :], start=True, stop=False)
                    pe.matmul(tail[:, cols], lhsT=wt1[:, 1, cols], rhs=gram[:, F, :], start=False, stop=False)
                    pe.matmul(tail[:, cols], lhsT=wt1[:, 2, cols], rhs=z2T[:, :], start=False, stop=False)
                    ins = pe.matmul(tail[:, cols], lhsT=wt1d[:, cols], rhs=dnT[:, :], start=False, stop=True)
                ins.then_inc(tail_ready, 1)

            def top2(k):
                wait(pe, tail_done, k * GU + NG + 3)
                for m in range(TOP2 // P):
                    cols = slice(m * P, (m + 1) * P)
                    for t in range(TOP1 // P):
                        ins = pe.matmul(tail[:, cols], lhsT=wt2[:, t, cols], rhs=h1T[:, t, :],
                                        start=(t == 0), stop=(t == TOP1 // P - 1))
                ins.then_inc(tail_ready, 1)

            def top3(k):
                wait(pe, tail_done, k * GU + NG + 4)
                for t in range(TOP2 // P):
                    ins = pe.matmul(tail[0:1, 0:P], lhsT=wt3[:, t:t + 1], rhs=h2T[:, t, :],
                                    start=(t == 0), stop=(t == TOP2 // P - 1))
                ins.then_inc(tail_ready, 1)

            def tail_steps(k, c, s, banks=(tail,)):
                if (c, s) in G_AT:
                    group(k, G_AT[c, s], banks)
                if (c, s) == DENSE_AT:
                    dense_transpose(k)
                if (c, s) in W2_AT:
                    layer2(k, W2_AT[c, s])
                if (c, s) == TOP1_AT:
                    top1(k)
                if (c, s) == TOP2_AT:
                    top2(k)
                if (c, s) == TOP3_AT:
                    top3(k)

            pe.wait_ge(w_lo, 2)
            x0_transpose_waits(0, 0)
            x0_transpose(0, 0)
            pair_transpose(0, 0, 0, tr[0])
            for t in range(T0):
                if t + 1 < T0:
                    pair_transpose(0, 0, t + 1, tr[(t + 1) % 2])
                layer0(0, 0, t)
            pe.wait_ge(w_hi, n)
            pe.wait_ge(w_lo, 2 + NB)
            pe.wait_ge(small_loaded, 16 * 9)

            def body(i):
                for c in range(CH):
                    ahead = not (last(i) and c == CH - 1)
                    for s in range(SLOTS):
                        if ahead and s == S_A:
                            x0_transpose_waits(i, c + 1)
                        t, off = divmod(s - S_B, EVERY)
                        if ahead and off == 0 and 0 <= t < T0:
                            pair_transpose(i, c + 1, t, tr_bank(c, "pair", t))
                        t, off = divmod(s - S_MM, EVERY)
                        if ahead and off == 0 and 0 <= t < T0:
                            layer0(i, c + 1, t)
                        if (c, s) in DIAG_AT:
                            diag_transpose_waits(i, DIAG_AT[c, s])
                        if not first(i):
                            tail_steps(i - 1, c, s)
                        layer1_bank(i, c, s)
                        if ahead and s == S_A:
                            x0_transpose(i, c + 1)
                        if (c, s) in DIAG_AT:
                            diag_transpose(i, DIAG_AT[c, s])

            iterations(pe, body)
            for c in range(CH):
                for s in range(SLOTS):
                    tail_steps(BT - 1, c, s, idle_banks)

        @block.scalar
        def _(act):
            banks = yd + ya
            act.wait_ge(wtr, 1)
            act.activation(w0hi[:, 0:4, :], banks[0][0:SPT * F, :].rearrange("p (t h) -> p t h", h=H),
                           ACT.Copy).then_inc(w_hi, 1)
            act.wait_ge(wtr, 2)
            short = T0 - 1
            act.activation(w0hi[:, 4:short, :], banks[1][0:SPT * F, 0:(short - 4) * P].rearrange("p (t h) -> p t h", h=H),
                           ACT.Copy)
            act.activation(w0hi[0:rows(short), short, :], banks[1][0:rows(short), (short - 4) * P:(T0 - 4) * P],
                           ACT.Copy).then_inc(w_hi, 1)

            def copy_fields(b):
                act.wait_ge(gathered, (b + 1) * (16 * F))
                view = e_land[:, :, :].rearrange("p f d -> p d f")
                act.activation(e_tr[:, :, 0:F], view, ACT.Copy).then_inc(e_copied, 1)
                act.activation(e_tr[:, :, F:FX], view[:, :, 0:FX - F], ACT.Copy).then_inc(e_copied, 1)

            def weights():
                n = 2
                for g in range(NB):
                    m = fields(g) * H
                    act.wait_ge(wtr, n + 1)
                    act.activation(w1hi[:, g * JB * H:g * JB * H + m], banks[n % 4][:, 0:m], ACT.Copy).then_inc(w_hi, 1)
                    n += 1
                for g in range(NB):
                    act.wait_ge(wtr, n + 1)
                    act.activation(w2T[:, g * JB:g * JB + fields(g), :],
                                   banks[n % 4][:, 0:fields(g) * H].rearrange("p (t h) -> p t h", h=H), ACT.Copy)\
                        .then_inc(w_hi, 1)
                    n += 1
                act.wait_ge(small_loaded, 16 * 9)
                act.activation(b2sum[:, :], b2c[:, :], ACT.Copy, scale=float(D)).then_inc(w_hi, 1)

            def x0_copies(i, c):
                q = i * CH + c
                cc = c % CH
                wait(act, x0_tr, q + 1)
                if cc == 0 and c == CH:
                    wait(act, tr_ready, tr_use(i, 2, "diag", 3) + 1)
                act.activation(x0bd[:, :, cc * DC:(cc + 1) * DC].rearrange("p b d -> p d b"),
                               l0[0:F, :].rearrange("p (d b) -> p d b", b=P), ACT.Copy).then_inc(x0_out, 1)
                wait(act, macs, (i * CH + c - CH + 1) * (DC * MACS) if not first(i) or c >= CH else 0)
                act.activation(e_sc[:, cc * DC:(cc + 1) * DC, :], e_tr[:, cc * DC:(cc + 1) * DC, 0:F],
                               ACT.Copy).then_inc(x0_out, 1)

            def pair_copy(i, c, t, use, bank):
                wait(act, tr_ready, use + 1)
                wait(act, l0_mm, (i * CH + c) * T0 + (t - P_SLOTS + 1))
                act.activation(pairs_hi[0:rows(t), (c * T0 + t) % P_SLOTS, :], bank[0:rows(t), :], ACT.Copy)\
                    .then_inc(pairs_rounded, 1)

            def diag_blocks(i, r, part):
                if part == 0:
                    wait(act, tr_ready, tr_use(i, 2, "diag", r) + 1)
                    if r == 0 and first(i):
                        wait(act, setup_done, 1)
                    elif r == 0:
                        wait(act, tail_ready, (i - 1) * GU + NG)
                x0 = tr_bank(2, "diag", r)[:, 0:4 * F].rearrange("p (g j) -> p g j", j=F)
                for b in range(4 * part, 4 * part + 4):
                    ins = act.activation(diag[:, 4 * r:4 * r + 4, b, 0:F], x0, ACT.Copy, scale=mask[:, b:b + 1])
                if part == 1:
                    ins.then_inc(diag_made, 1)

            def x1_copies(i, c):
                q = i * CH + c
                wait(act, l0_mm, (q + 1) * T0)
                wait(act, x1_split, q * 2)
                act.activation(x1f[:, :], l0[:, :], ACT.Identity, bias=b0c[:, :]).then_inc(x1_out, 1)
                wait(act, ya_ready, (q - CH + 1) * (DC * HALF))
                act.activation(x1hi[:, c % CH, :], l0[:, :], ACT.Identity, bias=b0c[:, :]).then_inc(x1_out, 1)

            def layer1_bank(i, c, s):
                dd, k = divmod(s, NB)
                u = c * DC + dd
                g = u * HALF + k // 2
                if s < NB and k == 1:
                    wait(act, x0_out, (i * CH + c + 1) * 2)
                wait(act, ya_ready, i * (D * HALF) + g + 1)
                before = g - PROD_SLOTS
                uu, kk = divmod(before, HALF)
                wait(act, prods_added, i * (D * (HALF - 1)) + (uu * (HALF - 1) + max(kk, 1)))
                for j in range(fields(k)):
                    ins = act.activation(prods[:, g % PROD_SLOTS, j * H:(j + 1) * H], ya[g % 2][:, j * H:(j + 1) * H],
                                         ACT.Copy, scale=e_sc[:, u, k * JB + j:k * JB + j + 1])
                ins.then_inc(prods_ready, 1)

            def tail_steps(k, c, s, banks=(tail,)):
                if (c, s - 1) in G_AT:
                    g = G_AT[c, s - 1]
                    wait(act, tail_ready, k * GU + g + 1)
                    act.activation(gram[:, :, 8 * g:8 * g + 8],
                                   banks[g % len(banks)][:, 0:8 * JX].rearrange("p (b j) -> p j b", j=JX), ACT.Copy).then_inc(tail_done, 1)
                if (c, s - 1) == DENSE_AT:
                    wait(act, tail_ready, k * GU + NG + 1)
                    act.activation(dnT[:, :], tail[0:ND, 0:P], ACT.Copy).then_inc(tail_done, 1)
                if (c, s - 2) == max(W2_AT):
                    wait(act, tail_ready, k * GU + NG + 2)
                    act.activation(z2T[:, :], tail[:, 0:P], ACT.Identity, bias=b2sum[:, :]).then_inc(tail_done, 1)
                if (c, s - 2) == TOP1_AT:
                    wait(act, tail_ready, k * GU + NG + 3)
                    for m in range(TOP1 // P):
                        ins = act.activation(h1T[:, m, :], tail[:, m * P:(m + 1) * P], ACT.Relu, bias=bt1[:, m:m + 1])
                    ins.then_inc(tail_done, 1)
                if (c, s - 1) == TOP2_AT:
                    wait(act, tail_ready, k * GU + NG + 4)
                    for m in range(TOP2 // P):
                        ins = act.activation(h2T[:, m, :], tail[:, m * P:(m + 1) * P], ACT.Relu, bias=bt2[:, m:m + 1])
                    ins.then_inc(tail_done, 1)
                if (c, s - 1) == TOP3_AT:
                    wait(act, tail_ready, k * GU + NG + 5)
                    wait(act, y_free, (k + 1) * 16)
                    act.activation(y_sb[:, :], tail[0:1, 0:P], ACT.Copy).then_inc(tail_done, 1)

            weights()
            copy_fields(0)
            x0_copies(0, 0)
            for t in range(T0):
                pair_copy(0, 0, t, t, tr[t % 2])
            x1_copies(0, 0)

            def body(i):
                for c in range(CH):
                    ahead = not (last(i) and c == CH - 1)
                    for s in range(SLOTS):
                        if ahead and s == S_A + 1:
                            x0_copies(i, c + 1)
                        if ahead and s == S_X1:
                            x1_copies(i, c + 1)
                        t, off = divmod(s - S_B - 1, EVERY)
                        if ahead and off == 0 and 0 <= t < T0:
                            pair_copy(i, c + 1, t, tr_use(i, c, "pair", t), tr_bank(c, "pair", t))
                        for part, after in enumerate(DIAG_PARTS):
                            if (c, s - after) in DIAG_AT:
                                diag_blocks(i, DIAG_AT[c, s - after], part)
                        if c == 2 and s == S_FIELDS and not last(i):
                            wait(act, pairs_made, (i + 1) * (CH * T0))
                            wait(act, x0_tr, (i + 1) * CH)
                            wait(act, x0_out, (i + 1) * (CH * 2))
                            copy_fields(i + 1)
                        if not first(i):
                            tail_steps(i - 1, c, s)
                        if s % 2 == 1:
                            layer1_bank(i, c, s)

            iterations(act, body)
            for c in range(CH):
                for s in range(SLOTS):
                    tail_steps(BT - 1, c, s, idle_banks)

        @block.vector
        def _(dve):
            def pair_products(i, c, t, use):
                if t == 0:
                    wait(dve, e_copied, (i + (1 + c // CH)) * 2)
                if use is not None:
                    wait(dve, tr_ready, use + 1)
                n = rows(t) // F
                x0 = e_tr[:, (c % CH) * DC:(c % CH) * DC + DC, :]
                one = bass.AP(tensor=x0.tensor, offset=x0.offset, ap=[x0.ap[0], [FX, DC], [0, n], [1, F]])
                other = bass.AP(tensor=x0.tensor, offset=x0.offset + SPT * t,
                                ap=[x0.ap[0], [FX, DC], [1, n], [1, F]])
                out = pairsT[:, :, SPT * F * t:SPT * F * t + rows(t)].rearrange("p d (s a) -> p d s a", a=F)
                dve.tensor_tensor(out, one, other, ALU.mult).then_inc(pairs_made, 1)

            dve.wait_ge(w0_loaded, 16 * 4)
            diagonal = w0x[:, :].rearrange("p (a r) -> p r a", r=FX + 1)
            for s in range(SHIFTS):
                dst = w0s[:, s * F:(s + 1) * F]
                if s == 0:
                    dve.tensor_copy(dst, diagonal[:, 0, :]).then_inc(w0_summed, 1)
                else:
                    other = w0y[:, s * F:s * F + (F + 1) * F].rearrange("p (a r) -> p r a", r=F + 1)[:, 0, :]
                    dve.tensor_tensor(dst, diagonal[:, s, :], other, ALU.add).then_inc(w0_summed, 1)

            banks = yd + ya
            for n, (t, count) in enumerate(((0, 4), (4, T0 - 5), (T0 - 1, 1))):
                bank, at = (banks[0], 0) if n == 0 else (banks[1], t - 4)
                dve.wait_ge(w_hi, min(n, 1) + 1)
                r = rows(t)
                ins = dve.tensor_tensor(w0lo[0:r, t:t + count, :],
                                        bank[0:r, at * P:(at + count) * P].rearrange("p (t h) -> p t h", h=H),
                                        w0hi[0:r, t:t + count, :].bitcast(F32), ALU.subtract)
                if n != 1:
                    ins.then_inc(w_lo, 1)
            for g in range(NB):
                dve.wait_ge(w_hi, 2 + g + 1)
                cols = slice(g * JB * H, (g * JB + fields(g)) * H)
                dve.tensor_tensor(w1lo[:, cols], banks[(2 + g) % 4][:, 0:fields(g) * H],
                                  w1hi[:, cols].bitcast(F32), ALU.subtract).then_inc(w_lo, 1)
            dve.wait_ge(consts_done, 5)
            dve.wait_ge(wtr, 2 + 2 * NB)
            dve.tensor_copy(diag[:, :, :, F], mask[:, :].rearrange("p (o b) -> p o b", o=1).to_broadcast([P, NG, 8]))\
                .then_inc(setup_done, 1)

            def pair_remainder(i, c, t, bank):
                wait(dve, pairs_rounded, (i * CH + c) * T0 + (t + 1))
                r, slot = rows(t), (c * T0 + t) % P_SLOTS
                dve.tensor_tensor(pairs_lo[0:r, slot, :], bank[0:r, :], pairs_hi[0:r, slot, :].bitcast(F32),
                                  ALU.subtract).then_inc(pairs_split, 1)

            def x1_remainder(i, c):
                q = i * CH + c
                wait(dve, x1_out, (q + 1) * 2)
                dve.tensor_tensor(x1lo[:, c % CH, :], x1f[:, :], x1hi[:, c % CH, :].bitcast(F32),
                                  ALU.subtract).then_inc(x1_split, 1)
                wait(dve, z0_done, i + (c // CH))
                dve.tensor_reduce(z0part[:, c % CH, :], x1f[:, :].rearrange("p (d b) -> p b d", b=P),
                                  AX.X, ALU.add).then_inc(x1_split, 1)

            def z0_total(i):
                if not first(i):
                    wait(dve, tail_ready, (i - 1) * GU + NG + 3)
                wait(dve, x1_split, (i + 1) * (2 * CH))
                dve.tensor_reduce(z0T[:, :], z0part[:, :, :].rearrange("p c b -> p b c"), AX.X, ALU.add)\
                    .then_inc(z0_done, 1)

            def layer1_bank(i, c, s):
                dd, k = divmod(s, NB)
                u = c * DC + dd
                g = u * HALF + k // 2
                if s == 0:
                    wait(dve, x0_out, (i * CH + c + 1) * 2)
                wait(dve, yd_ready, i * (D * HALF) + g + 1)
                if k == 0:
                    wait(dve, ab_ready, i * D + (u - 1))
                for j in range(JB):
                    m = (k // 2) * JB + j
                    a = acc[:, u % 2, m % 2, :]
                    y = yd[g % 2][:, j * H:(j + 1) * H]
                    x = e_sc[:, u, k * JB + j:k * JB + j + 1]
                    if m == 0:
                        ins = dve.scalar_tensor_tensor(a, y, x, b1rep[:, :], ALU.mult, ALU.add)
                    elif m == 1:
                        ins = dve.tensor_scalar(a, y, x, None, ALU.mult)
                    else:
                        wait(dve, macs, i * (D * MACS) + (u * MACS + m - 1))
                        ins = dve.scalar_tensor_tensor(a, y, x, a, ALU.mult, ALU.add)
                    ins.then_inc(macs, 1)
                if k == NB - 2:
                    wait(dve, macs, i * (D * MACS) + (u + 1) * MACS)
                    wait(dve, x2_ready, i * D + (u - 1))
                    dve.tensor_tensor(ab[:, u % 2, :], acc[:, u % 2, 0, :], acc[:, u % 2, 1, :], ALU.add)\
                        .then_inc(ab_ready, 1)

            dve.wait_ge(wtr, 2)
            for t in range(T0):
                pair_products(0, 0, t, None)
                if t >= 2:
                    pair_remainder(0, 0, t - 2, tr[t % 2])
            for t in range(T0 - 2, T0):
                pair_remainder(0, 0, t, tr[t % 2])
            x1_remainder(0, 0)
            for t in range(T0):
                pair_products(0, 1, t, t)

            def body(i):
                for c in range(CH):
                    ahead = not (last(i) and c == CH - 1)
                    for s in range(SLOTS):
                        t, off = divmod(s - S_B - 2, EVERY)
                        if ahead and off == 0 and 0 <= t < T0:
                            pair_remainder(i, c + 1, t, tr_bank(c, "pair", t))
                        if s in S_PAIRS[c] and not (last(i) and c >= 2):
                            t = S_PAIRS[c].index(s)
                            pair_products(i, c + 2, t, tr_use(i, c, "pair", t))
                        if (c, s) == (3, 14):
                            z0_total(i)
                        if ahead and s == S_XL:
                            x1_remainder(i, c + 1)
                        if s % 2 == 0:
                            layer1_bank(i, c, s)

            iterations(dve, body)


def kernel(**inputs):
    import numpy as _np
    import concourse.bacc as _bacc
    from concourse import mybir as _mybir
    from concourse.bass_utils import run_bass_kernel_spmd as _run

    nc = _bacc.Bacc("TRN2", target_bir_lowering=False, num_devices=1)
    arrays, aps = {}, {}
    for name, value in inputs.items():
        a = _np.ascontiguousarray(value)
        arrays[f"in_{name}"] = a
        aps[name] = nc.dram_tensor(f"in_{name}", a.shape, _mybir.dt.from_np(a.dtype), kind="ExternalInput").ap()
    out = nc.dram_tensor("out_y", (B, 1), F32, kind="ExternalOutput").ap()
    cin_tower(nc, aps["dense_ctx"], aps["ids"], [aps[f"tbl_{f}"] for f in range(F)],
              aps["W_top1"], aps["b_top1"], aps["W_top2"], aps["b_top2"], aps["W_top3"],
              aps["L0_rec_W0"], aps["L0_rec_b0"], aps["L0_rec_W1"], aps["L0_rec_b1"],
              aps["L0_rec_W2"], aps["L0_rec_b2"], out)
    r = _run(nc, [arrays], core_ids=[0])
    return r.results[0]["out_y"]
```

```python
import concourse.bass as bass
from concourse import mybir
from contextlib import ExitStack

F32 = mybir.dt.float32
F32R = mybir.dt.float32r
I32 = mybir.dt.int32
ALU = mybir.AluOpType
ACT = mybir.ActivationFunctionType
AX = mybir.AxisListType

P = 128
B = 1024
F = 39
D = 16
H = 128
BT = B // P
DC = 4
CH = D // DC
SHIFTS = (F + 1) // 2
SPT = 3
T0 = -(-SHIFTS // SPT)
FX = F + SHIFTS - 1
JB = 4
NB = -(-F // JB)
HALF = NB // 2
MACS = HALF * JB
PROD_SLOTS = 5
P_SLOTS = 2
B_SLOTS = 4
X2_SLOTS = 2
NG = P // 8
JX = F + 1
GU = NG + 5
TOP1, TOP2, ND = 512, 256, 16
SLOTS = DC * NB

S_PAIR, S_MM, EVERY = 0, 6, 4
S_X1, S_XL = 32, 34
S_X0, S_X0_OUT = 28, (29, 35, 37)
S_FIELDS = 20
G_AT = {((20 + 4 * g) // SLOTS, (20 + 4 * g) % SLOTS): g for g in range(NG)}
DENSE_AT = (2, 4)
W2_AT = {(2, 11 + 2 * n): n for n in range(13)}
TOP1_AT, TOP2_AT, TOP3_AT = (3, 3), (3, 13), (3, 18)
DIAG_AT = {(2, 2 + 7 * r): r for r in range(4)}
DIAG_PARTS = (1, 3)


GATHERS = 3
EARLY = 5
EARLY_FIELDS = GATHERS * EARLY


def transposed_bank_order():
    order = {}
    for c in range(CH):
        steps = [(S_PAIR + EVERY * t, "pair", t) for t in range(T0)] + [(S_X0, "x0", 0)]
        steps += [(s, "diag", r) for (cc, s), r in DIAG_AT.items() if cc == c]
        for _, kind, n in sorted(steps):
            order[c, kind, n] = len(order)
    return order


TR_ORDER = transposed_bank_order()
TR_PER_ITER = len(TR_ORDER)


def cin_tower(nc, dense_ctx, ids, tables, W_top1, b_top1, W_top2, b_top2, W_top3,
              W0, b0, W1, b1, W2, b2, out):
    x0_dram = nc.dram_tensor("x0_scratch", (FX, DC * P), F32, kind="Internal").ap()
    x2_dram = nc.dram_tensor("x2_scratch", (P * D, H), F32, kind="Internal").ap()
    ctx = ExitStack()
    with ctx:
        def sb(name, shape, dt=F32):
            return ctx.enter_context(nc.sbuf_tensor(name, shape, dt))

        def pb(name):
            return ctx.enter_context(nc.psum_tensor(name, [P, 512], F32))

        def sem(name):
            return ctx.enter_context(nc.semaphore(name))

        ident = sb("ident", [P, P])
        mask = sb("mask", [P, 8])
        ids_sb = sb("ids_sb", [P, F], I32)
        e_land = sb("e_land", [P, F, D])
        e_tr = sb("e_tr", [P, D, F])
        e_sc = sb("e_sc", [P, D, F])
        x0c = sb("x0c", [F, DC * P])
        x0a = sb("x0a", [SPT * F, DC * P])
        x0s = sb("x0s", [P, B_SLOTS, DC * P])
        x0bd = sb("x0bd", [F, P, D])
        pairs_hi = sb("pairs_hi", [SPT * F, P_SLOTS, 512], F32R)
        pairs_lo = sb("pairs_lo", [SPT * F, P_SLOTS, 512], F32R)
        w0s = x0s[:, :, :].rearrange("p n c -> p (n c)")[:, 0:SHIFTS * F]
        w0hi = sb("w0hi", [SPT * F, T0, H], F32R)
        w0lo = sb("w0lo", [SPT * F, T0, H], F32R)
        x1f = sb("x1f", [P, 512])
        x1hi = sb("x1hi", [P, CH, 512], F32R)
        x1lo = sb("x1lo", [P, CH, 512], F32R)
        z0part = sb("z0part", [P, CH, P])
        w1hi = sb("w1hi", [P, F * H], F32R)
        w1lo = sb("w1lo", [P, F * H], F32R)
        w2T = sb("w2T", [P, F, H])
        prods = sb("prods", [P, PROD_SLOTS, JB * H])
        acc = sb("acc", [P, 2, 2, H])
        ab = sb("ab", [P, 2, H])
        psum4 = sb("psum4", [P, JB * H])
        psum2 = sb("psum2", [P, 2 * H])
        psum1 = sb("psum1", [P, H])
        x2t = sb("x2t", [P, X2_SLOTS, H])
        x2g = sb("x2g", [P, NG, H])
        diag = sb("diag", [P, NG, 8, JX])
        gram = sb("gram", [P, JX, P])
        w1raw = gram[:, :, :].rearrange("p j b -> p (j b)")
        w2raw = diag[:, :, :, :].rearrange("p g b j -> p (g b j)")
        W0N = (FX + 1) * F
        w0x = w2raw[:, 0:W0N]
        w0y = w2raw[:, W0N:2 * W0N]
        b0c = sb("b0c", [P, 1])
        b1rep = sb("b1rep", [P, H])
        b2c = sb("b2c", [P, 1])
        b2sum = sb("b2sum", [P, 1])
        bt1 = sb("bt1", [P, TOP1 // P])
        bt2 = sb("bt2", [P, TOP2 // P])
        wt1 = sb("wt1", [P, 3, TOP1])
        wt1d = sb("wt1d", [ND, TOP1])
        wt2 = sb("wt2", [P, TOP1 // P, TOP2])
        wt3 = sb("wt3", [P, TOP2 // P])
        z0T = sb("z0T", [P, P])
        z2T = sb("z2T", [P, P])
        dn = sb("dn", [P, ND])
        dnT = sb("dnT", [ND, P])
        h1T = sb("h1T", [P, TOP1 // P, P])
        h2T = sb("h2T", [P, TOP2 // P, P])
        y_sb = sb("y_sb", [1, P])

        yd = [pb("yd0"), pb("yd1")]
        ya = [pb("ya0"), pb("ya1")]
        tr = [pb("tr0"), pb("tr1")]
        l0 = pb("l0")
        tail = pb("tail")

        consts_done = sem("consts_done")
        w0_loaded = sem("w0_loaded")
        w1_loaded = sem("w1_loaded")
        w2_loaded = sem("w2_loaded")
        small_loaded = sem("small_loaded")
        w0_summed = sem("w0_summed")
        wtr = sem("wtr")
        w_hi = sem("w_hi")
        w_lo = sem("w_lo")
        setup_done = sem("setup_done")
        ids_loaded = sem("ids_loaded")
        gathered = sem("gathered")
        e_copied = sem("e_copied")
        x0_tr = sem("x0_tr")
        x0_out = sem("x0_out")
        x0_stored = sem("x0_stored")
        a_loaded = sem("a_loaded")
        b_loaded = [sem(f"b_loaded{n}") for n in range(B_SLOTS)]
        pairs_made = sem("pairs_made")
        diag_tr = sem("diag_tr")
        pairs_rounded = sem("pairs_rounded")
        pairs_split = sem("pairs_split")
        diag_made = sem("diag_made")
        l0_mm = sem("l0_mm")
        x1_out = sem("x1_out")
        x1_split = sem("x1_split")
        z0_done = sem("z0_done")
        yd_ready = sem("yd_ready")
        ya_ready = sem("ya_ready")
        macs = sem("macs")
        ab_ready = sem("ab_ready")
        prods_ready = sem("prods_ready")
        prods_added = sem("prods_added")
        folded = sem("folded")
        x2_ready = sem("x2_ready")
        x2_stored = [sem(f"x2_stored{n}") for n in range(X2_SLOTS)]
        x2_loaded = [sem("x2_loaded0"), sem("x2_loaded1")]
        dense_loaded = sem("dense_loaded")
        tail_ready = sem("tail_ready")
        tail_done = sem("tail_done")
        y_free = sem("y_free")

        idle_banks = (tail, tr[0], tr[1], l0)

        block = ctx.enter_context(nc.Block())

        def wait(eng, s, value):
            if not isinstance(value, int) or value > 0:
                eng.wait_ge(s, value)

        def iterations(eng, body, ends=1):
            body(0)
            with eng.Fori(1, BT - ends) as i:
                body(i)
            for i in range(BT - ends, BT):
                body(i)

        def first(i):
            return isinstance(i, int) and i == 0

        def last(i):
            return isinstance(i, int) and i == BT - 1

        def more(i, n):
            return not isinstance(i, int) or i + n < BT

        def tr_bank(c, kind, n):
            return tr[(T0 + 2 + TR_ORDER[c, kind, n]) % 2]

        def wait_tr_free(eng, i, c, kind, n):
            before = TR_ORDER[c, kind, n] - 2
            ago = 1 if before < 0 else 0
            cc, kk, nn = next(key for key, use in TR_ORDER.items() if use == before + ago * TR_PER_ITER)
            cc -= ago * CH
            if kk == "pair":
                wait(eng, pairs_split, i * (CH * T0) + ((cc + 1) * T0 + nn + 1))
            elif kk == "x0":
                wait(eng, x0_out, i * (3 * CH) + ((cc + 2) * 3 + 2))
            else:
                wait(eng, diag_made, i * 4 + nn + 1)

        def rows(t):
            return (min(SHIFTS, SPT * (t + 1)) - SPT * t) * F

        def fields(k):
            return min(JB, F - JB * k)

        @block.sync
        def _(sp):
            def ahead_of_wait(*values):
                for v in values:
                    if not isinstance(v, int):
                        sp.lower_val(v)
                return values

            def load_ids(b):
                row, reads = ahead_of_wait(b * P, b * (16 * F))
                wait(sp, gathered, reads)
                sp.dma_start(ids_sb[:, :], ids[bass.ds(row, P), :]).then_inc(ids_loaded, 16)

            load_ids(0)
            w0v = W0.rearrange("h (a k) -> h a k", k=F)
            w0xv = w0x[:, 0:FX * F].rearrange("p (a k) -> p a k", k=FX)
            sp.dma_start(w0xv[:, :, 0:F], w0v).then_inc(w0_loaded, 16)
            sp.dma_start(w0xv[:, :, F:FX], w0v[:, :, 0:FX - F]).then_inc(w0_loaded, 16)
            sp.dma_start(w0y[:, 0:F * F], W0).then_inc(w0_loaded, 16)
            sp.dma_start(w0y[:, F * F:FX * F], W0[:, 0:(FX - F) * F]).then_inc(w0_loaded, 16)
            sp.dma_start(w1raw[:, 0:F * H], W1).then_inc(w1_loaded, 16)
            with nc.allow_non_contiguous_dma(reason="biases and the last layer's weights, once"):
                sp.dma_start(b0c[:, :], b0.rearrange("(p o) -> p o", o=1)).then_inc(small_loaded, 16)
                sp.dma_start(b1rep[:, :], b1.rearrange("(o h) -> o h", o=1).to_broadcast([P, H])).then_inc(small_loaded, 16)
                sp.dma_start(b2c[:, :], b2.rearrange("(p o) -> p o", o=1)).then_inc(small_loaded, 16)
                sp.dma_start(bt1[:, :], b_top1.rearrange("(m p) -> p m", p=P)).then_inc(small_loaded, 16)
                sp.dma_start(bt2[:, :], b_top2.rearrange("(m p) -> p m", p=P)).then_inc(small_loaded, 16)
                sp.dma_start(wt3[:, :], W_top3.rearrange("(m p) o -> p (m o)", p=P)).then_inc(small_loaded, 16)
            sp.dma_start(wt1[:, :, :], W_top1[0:3 * H, :].rearrange("(k p) n -> p k n", p=P)).then_inc(small_loaded, 16)
            sp.dma_start(wt1d[:, :], W_top1[3 * H:3 * H + ND, :]).then_inc(small_loaded, 16)
            sp.dma_start(wt2[:, :, :], W_top2.rearrange("(k p) n -> p k n", p=P)).then_inc(small_loaded, 16)

            sp.wait_ge(w0_summed, SHIFTS)
            sp.dma_start(w2raw[:, 0:F * H], W2).then_inc(w2_loaded, 16)

            x2_rows = x2_dram.rearrange("(b d) k -> b d k", d=D)

            def load_dense(k):
                sp.dma_start(dn[:, :], dense_ctx[bass.ds(k * P, P), :]).then_inc(dense_loaded, 16)

            def store_y(k):
                sp.dma_start(out[bass.ds(k * P, P), :].rearrange("b o -> o b"), y_sb[:, :]).then_inc(y_free, 16)

            def store_x0(i, c):
                q = i * CH + c
                copied, made = ahead_of_wait(i * (3 * CH) + (c * 3 + 1), i * (CH * T0) + c * T0)
                wait(sp, pairs_made, made)
                wait(sp, x0_out, copied)
                sp.dma_start(x0_dram[0:F, :], x0c[:, :]).then_inc(x0_stored, 16)
                sp.dma_start(x0_dram[F:FX, :], x0c[0:FX - F, :]).then_inc(x0_stored, 16)

            def load_x0a(i, c):
                stores, = ahead_of_wait(i * (32 * CH) + (c + 1) * 32)
                wait(sp, x0_stored, stores)
                sp.dma_start(x0a[:, :], bass.AP(tensor=x0_dram.tensor, offset=x0_dram.offset,
                                                ap=[[0, SPT], [DC * P, F], [1, DC * P]])).then_inc(a_loaded, 16)

            def load_x0s(i, c, t):
                m = c * T0 + t
                made, = ahead_of_wait(i * (CH * T0) + (m - B_SLOTS + 1))
                wait(sp, pairs_made, made)
                slot = m % B_SLOTS
                sp.dma_start(x0s[0:rows(t), slot, :],
                             bass.AP(tensor=x0_dram.tensor, offset=x0_dram.offset + SPT * t * DC * P,
                                     ap=[[DC * P, rows(t) // F], [DC * P, F], [1, DC * P]])).then_inc(b_loaded[slot], 16)

            load_ids(1)
            sp.wait_ge(wtr, 2)
            store_x0(0, 0)
            load_x0a(0, 0)
            for t in range(T0):
                load_x0s(0, 0, t)
            store_x0(0, 1)
            load_x0a(0, 1)
            for t in range(B_SLOTS):
                load_x0s(0, 1, t)

            def body(i):
                if not first(i):
                    load_dense(i - 1)
                for u in range(D):
                    if u == D - EARLY - 1 and more(i, 2):
                        load_ids(i + 2)
                    c, dd = divmod(u, DC)
                    if dd < 2 and not (last(i) and c == CH - 1):
                        for t in ((4, 5), (6,))[dd]:
                            load_x0s(i, c + 1, t)
                    if dd == 2 and not (last(i) and c >= CH - 2):
                        store_x0(i, c + 2)
                        load_x0a(i, c + 2)
                        for t in range(B_SLOTS):
                            load_x0s(i, c + 2, t)
                    loads, tiles = ahead_of_wait(i * 16, i * D + u + 1)
                    if u == 0 and not first(i):
                        wait(sp, x2_loaded[0], loads)
                        wait(sp, x2_loaded[1], loads)
                    wait(sp, x2_ready, tiles)
                    sp.dma_start(x2_rows[:, u, :], x2t[:, u % X2_SLOTS, :]).then_inc(x2_stored[u % X2_SLOTS], 16)
                stores, uses = ahead_of_wait((i + 1) * (16 * D // X2_SLOTS), i * GU)
                for n in range(X2_SLOTS):
                    wait(sp, x2_stored[n], stores)
                if not first(i):
                    wait(sp, tail_done, uses)
                for n in range(2):
                    half = slice(n * NG // 2, (n + 1) * NG // 2)
                    sp.dma_start(x2g[:, half, :], x2_dram.rearrange("(g r) k -> r g k", r=P)[:, half, :])\
                        .then_inc(x2_loaded[n], 16)
                if not first(i):
                    store_y(i - 1)

            iterations(sp, body, ends=2)
            load_dense(BT - 1)
            sp.wait_ge(tail_done, BT * GU)
            store_y(BT - 1)
            sp.wait_ge(y_free, 16 * (BT + 1))

        @block.gpsimd
        def _(pool):
            pool.memset(y_sb[:, :], 0.0).then_inc(y_free, 16)
            pool.memset(ident[:, :], 0.0).then_inc(consts_done, 1)
            pool.memset(mask[:, :], 1.0).then_inc(consts_done, 1)
            pool.wait_ge(consts_done, 2)
            pool.affine_select(out=ident[:, :], in_=ident[:, :], compare_op=ALU.not_equal, fill=1.0,
                               base=0, pattern=[[-1, P]], channel_multiplier=1).then_inc(consts_done, 1)
            pool.affine_select(out=mask[:, :], in_=mask[:, :], compare_op=ALU.is_ge, fill=0.0,
                               base=0, pattern=[[-D, 8]], channel_multiplier=1).then_inc(consts_done, 1)
            pool.wait_ge(consts_done, 4)
            pool.affine_select(out=mask[:, :], in_=mask[:, :], compare_op=ALU.is_ge, fill=0.0,
                               base=D - 1, pattern=[[D, 8]], channel_multiplier=-1).then_inc(consts_done, 1)

            def gather(f):
                pool.indirect_dma_start(out=e_land[:, f, :], out_offset=None, in_=tables[f],
                                        in_offset=bass.IndirectOffsetOnAxis(ap=ids_sb[:, f:f + 1], axis=0),
                                        ).then_inc(gathered, 16)

            pool.wait_ge(ids_loaded, 16)
            for f in range(F):
                gather(f)
            pool.wait_ge(ids_loaded, 32)
            pool.wait_ge(e_copied, 1)
            for f in range(EARLY_FIELDS):
                gather(f)

            def add_banks(i, u):
                for e in range(HALF - 1):
                    wait(pool, prods_ready, i * (D * HALF) + (u * HALF + e + 2))
                    wait(pool, prods_added, i * (D * (HALF - 1)) + (u * (HALF - 1) + e))
                    n = JB * H if e + 2 < HALF else fields(NB - 1) * H
                    left = prods[:, (u * HALF) % PROD_SLOTS, 0:n] if e == 0 else psum4[:, 0:n]
                    pool.tensor_tensor(psum4[:, 0:n], left, prods[:, (u * HALF + e + 1) % PROD_SLOTS, 0:n],
                                       ALU.add).then_inc(prods_added, 1)

            def finish_tile(i, u):
                wait(pool, prods_added, i * (D * (HALF - 1)) + ((u + 1) * (HALF - 1)))
                pool.tensor_tensor(psum2[:, :], psum4[:, 0:2 * H], psum4[:, 2 * H:4 * H], ALU.add).then_inc(folded, 1)
                wait(pool, folded, i * (2 * D) + (2 * u + 1))
                pool.tensor_tensor(psum1[:, :], psum2[:, 0:H], psum2[:, H:2 * H], ALU.add).then_inc(folded, 1)
                wait(pool, folded, i * (2 * D) + (2 * u + 2))
                wait(pool, ab_ready, i * D + (u + 1))
                wait(pool, x2_stored[u % X2_SLOTS], (i * (D // X2_SLOTS) + u // X2_SLOTS) * 16)
                pool.tensor_tensor(x2t[:, u % X2_SLOTS, :], psum1[:, :], ab[:, u % 2, :], ALU.add).then_inc(x2_ready, 1)

            def body(i):
                for u in range(D):
                    if u == D - EARLY and more(i, 2):
                        wait(pool, ids_loaded, (i + 3) * 16)
                        wait(pool, e_copied, i + 2)
                    add_banks(i, u)
                    if u >= D - EARLY and more(i, 2):
                        for n in range(GATHERS):
                            gather((u - D + EARLY) * GATHERS + n)
                    if more(i, 1):
                        for f in range(EARLY_FIELDS + u * GATHERS, min(EARLY_FIELDS + (u + 1) * GATHERS, F)):
                            gather(f)
                    finish_tile(i, u)

            iterations(pool, body, ends=2)

        @block.tensor
        def _(pe):
            pe.wait_ge(consts_done, 3)
            banks = yd + ya
            n = 0

            def transpose_weights(raw, cols, count):
                nonlocal n
                for g in range(0, count, 4):
                    if n >= 4:
                        if n - 4 < 2 + NB:
                            pe.wait_ge(w_lo, n - 3)
                        else:
                            pe.wait_ge(w_hi, n - 3)
                    for t in range(g, min(g + 4, count)):
                        m = cols(t)
                        ins = pe.transpose(banks[n % 4][0:m.stop - m.start, (t - g) * P:(t - g + 1) * P],
                                           raw[:, m], ident[:, :])
                    ins.then_inc(wtr, 1)
                    n += 1

            pe.wait_ge(w0_summed, SHIFTS)
            transpose_weights(w0s, lambda t: slice(SPT * F * t, SPT * F * t + rows(t)), T0)
            pe.wait_ge(w1_loaded, 16)
            transpose_weights(w1raw, lambda t: slice(H * t, H * t + H), F)
            pe.wait_ge(w2_loaded, 16)
            transpose_weights(w2raw, lambda t: slice(H * t, H * t + H), F)

            def x0_transpose_waits(i, c):
                wait_tr_free(pe, i, c - 2, "x0", 0)
                wait(pe, e_copied, i + (1 + c // CH))

            def diag_transpose_waits(i, r):
                wait(pe, x0_out, i * (3 * CH) + (3 * CH - 1))
                wait_tr_free(pe, i, 2, "diag", r)

            def x0_transpose(c, bank):
                for d in range(DC):
                    ins = pe.transpose(bank[0:F, d * P:(d + 1) * P], e_tr[:, (c % CH) * DC + d, :], ident[:, :])
                ins.then_inc(x0_tr, 1)

            def layer0(i, c, t):
                q = i * CH + c
                if t == 0:
                    wait(pe, x1_out, q * 2)
                wait(pe, pairs_split, q * T0 + (t + 1))
                slot = (c * T0 + t) % P_SLOTS
                hi, lo = pairs_hi[0:rows(t), slot, :], pairs_lo[0:rows(t), slot, :]
                whi, wlo = w0hi[0:rows(t), t, :], w0lo[0:rows(t), t, :]
                pe.matmul(l0[:, :], lhsT=whi, rhs=hi, start=(t == 0), stop=False)
                pe.matmul(l0[:, :], lhsT=wlo, rhs=hi, start=False, stop=False)
                pe.matmul(l0[:, :], lhsT=whi, rhs=lo, start=False, stop=(t == T0 - 1)).then_inc(l0_mm, 1)

            def diag_transpose(i, r):
                bank = tr_bank(2, "diag", r)
                for g in range(4):
                    rows_bd = x0bd[:, (4 * r + g) * 8:(4 * r + g + 1) * 8, :].rearrange("p b d -> p (b d)")
                    ins = pe.transpose(bank[:, g * F:(g + 1) * F], rows_bd, ident[0:F, 0:F])
                ins.then_inc(diag_tr, 1)

            def layer1_bank(i, c, s):
                dd, k = divmod(s, NB)
                u = c * DC + dd
                if s == 0:
                    wait(pe, x1_split, (i * CH + c) * 2 + 1)
                g = u * HALF + k // 2
                cols = slice(k * JB * H, (k * JB + fields(k)) * H)
                n = fields(k) * H
                if k % 2 == 0:
                    wait(pe, macs, i * (D * MACS) + (g - 1) * JB)
                    bank, ready = yd[g % 2], yd_ready
                else:
                    wait(pe, prods_ready, i * (D * HALF) + (g - 1))
                    bank, ready = ya[g % 2], ya_ready
                hi = x1hi[:, c, dd * P:(dd + 1) * P]
                lo = x1lo[:, c, dd * P:(dd + 1) * P]
                pe.matmul(bank[:, 0:n], lhsT=hi, rhs=w1hi[:, cols], start=True, stop=False)
                pe.matmul(bank[:, 0:n], lhsT=hi, rhs=w1lo[:, cols], start=False, stop=False)
                pe.matmul(bank[:, 0:n], lhsT=lo, rhs=w1hi[:, cols], start=False, stop=True).then_inc(ready, 1)

            def group(k, g, banks=(tail,)):
                if g % (NG // 2) == 0:
                    wait(pe, x2_loaded[2 * g // NG], (k + 1) * 16)
                if g == 0:
                    wait(pe, diag_made, (k + 1) * 4)
                    wait(pe, setup_done, 1)
                if g >= len(banks):
                    wait(pe, tail_done, k * GU + (g - len(banks) + 1))
                pe.matmul(banks[g % len(banks)][:, 0:8 * JX], lhsT=x2g[:, g, :],
                          rhs=diag[:, g, :, :].rearrange("p b j -> p (b j)"),
                          start=True, stop=True).then_inc(tail_ready, 1)

            def dense_transpose(k):
                wait(pe, dense_loaded, (k + 1) * 16)
                wait(pe, tail_done, k * GU + NG)
                pe.transpose(tail[0:ND, 0:P], dn[:, :], ident[:, :]).then_inc(tail_ready, 1)

            def layer2(k, n):
                if n == 0:
                    wait(pe, tail_done, k * GU + NG + 1)
                for j in range(3 * n, 3 * n + 3):
                    ins = pe.matmul(tail[:, 0:P], lhsT=w2T[:, j, :], rhs=gram[:, j, :],
                                    start=(j == 0), stop=(j == F - 1))
                if n == F // 3 - 1:
                    ins.then_inc(tail_ready, 1)

            def top1(k):
                wait(pe, z0_done, k + 1)
                wait(pe, tail_done, k * GU + NG + 2)
                for m in range(TOP1 // P):
                    cols = slice(m * P, (m + 1) * P)
                    pe.matmul(tail[:, cols], lhsT=wt1[:, 0, cols], rhs=z0T[:, :], start=True, stop=False)
                    pe.matmul(tail[:, cols], lhsT=wt1[:, 1, cols], rhs=gram[:, F, :], start=False, stop=False)
                    pe.matmul(tail[:, cols], lhsT=wt1[:, 2, cols], rhs=z2T[:, :], start=False, stop=False)
                    ins = pe.matmul(tail[:, cols], lhsT=wt1d[:, cols], rhs=dnT[:, :], start=False, stop=True)
                ins.then_inc(tail_ready, 1)

            def top2(k):
                wait(pe, tail_done, k * GU + NG + 3)
                for m in range(TOP2 // P):
                    cols = slice(m * P, (m + 1) * P)
                    for t in range(TOP1 // P):
                        ins = pe.matmul(tail[:, cols], lhsT=wt2[:, t, cols], rhs=h1T[:, t, :],
                                        start=(t == 0), stop=(t == TOP1 // P - 1))
                ins.then_inc(tail_ready, 1)

            def top3(k):
                wait(pe, tail_done, k * GU + NG + 4)
                for t in range(TOP2 // P):
                    ins = pe.matmul(tail[0:1, 0:P], lhsT=wt3[:, t:t + 1], rhs=h2T[:, t, :],
                                    start=(t == 0), stop=(t == TOP2 // P - 1))
                ins.then_inc(tail_ready, 1)

            def tail_steps(k, c, s, banks=(tail,)):
                if (c, s) in G_AT:
                    group(k, G_AT[c, s], banks)
                if (c, s) == DENSE_AT:
                    dense_transpose(k)
                if (c, s) in W2_AT:
                    layer2(k, W2_AT[c, s])
                if (c, s) == TOP1_AT:
                    top1(k)
                if (c, s) == TOP2_AT:
                    top2(k)
                if (c, s) == TOP3_AT:
                    top3(k)

            pe.wait_ge(w_lo, 2)
            pe.wait_ge(e_copied, 1)
            x0_transpose(0, tr[0])
            for t in range(T0):
                layer0(0, 0, t)
            pe.wait_ge(pairs_split, T0 - 1)
            x0_transpose(1, tr[0])
            pe.wait_ge(w_hi, n)
            pe.wait_ge(w_lo, 2 + NB)
            pe.wait_ge(small_loaded, 16 * 9)

            def body(i):
                for c in range(CH):
                    ahead = not (last(i) and c == CH - 1)
                    for s in range(SLOTS):
                        if s == S_X0 and not (last(i) and c >= CH - 2):
                            x0_transpose_waits(i, c + 2)
                        t, off = divmod(s - S_MM, EVERY)
                        if ahead and off == 0 and 0 <= t < T0:
                            layer0(i, c + 1, t)
                        if (c, s) in DIAG_AT:
                            diag_transpose_waits(i, DIAG_AT[c, s])
                        if not first(i):
                            tail_steps(i - 1, c, s)
                        layer1_bank(i, c, s)
                        if s == S_X0 and not (last(i) and c >= CH - 2):
                            x0_transpose(c + 2, tr_bank(c, "x0", 0))
                        if (c, s) in DIAG_AT:
                            diag_transpose(i, DIAG_AT[c, s])

            iterations(pe, body)
            for c in range(CH):
                for s in range(SLOTS):
                    tail_steps(BT - 1, c, s, idle_banks)

        @block.scalar
        def _(act):
            banks = yd + ya
            act.wait_ge(wtr, 1)
            act.activation(w0hi[:, 0:4, :], banks[0][0:SPT * F, :].rearrange("p (t h) -> p t h", h=H),
                           ACT.Copy).then_inc(w_hi, 1)
            act.wait_ge(wtr, 2)
            short = T0 - 1
            act.activation(w0hi[:, 4:short, :], banks[1][0:SPT * F, 0:(short - 4) * P].rearrange("p (t h) -> p t h", h=H),
                           ACT.Copy)
            act.activation(w0hi[0:rows(short), short, :], banks[1][0:rows(short), (short - 4) * P:(T0 - 4) * P],
                           ACT.Copy).then_inc(w_hi, 1)

            def copy_fields(b):
                act.wait_ge(gathered, (b + 1) * (16 * F))
                act.activation(e_tr[:, :, :], e_land[:, :, :].rearrange("p f d -> p d f"), ACT.Copy).then_inc(e_copied, 1)

            def weights():
                n = 2
                for g in range(NB):
                    m = fields(g) * H
                    act.wait_ge(wtr, n + 1)
                    act.activation(w1hi[:, g * JB * H:g * JB * H + m], banks[n % 4][:, 0:m], ACT.Copy).then_inc(w_hi, 1)
                    n += 1
                for g in range(NB):
                    act.wait_ge(wtr, n + 1)
                    act.activation(w2T[:, g * JB:g * JB + fields(g), :],
                                   banks[n % 4][:, 0:fields(g) * H].rearrange("p (t h) -> p t h", h=H), ACT.Copy)\
                        .then_inc(w_hi, 1)
                    n += 1
                act.wait_ge(small_loaded, 16 * 9)
                act.activation(b2sum[:, :], b2c[:, :], ACT.Copy, scale=float(D)).then_inc(w_hi, 1)

            def x0_copies(i, c, part, bank):
                cc = c % CH
                if part == 0:
                    wait(act, x0_tr, i * CH + (c + 1))
                    wait(act, x0_stored, i * (32 * CH) + c * 32)
                    act.activation(x0c[:, :], bank[0:F, :], ACT.Copy).then_inc(x0_out, 1)
                elif part == 1:
                    if c == CH:
                        wait(act, diag_tr, (i + 1) * 4)
                    act.activation(x0bd[:, :, cc * DC:(cc + 1) * DC].rearrange("p b d -> p d b"),
                                   bank[0:F, :].rearrange("p (d b) -> p d b", b=P), ACT.Copy).then_inc(x0_out, 1)
                else:
                    wait(act, macs, (i * CH + c - CH + 1) * (DC * MACS) if not first(i) or c >= CH else 0)
                    act.activation(e_sc[:, cc * DC:(cc + 1) * DC, :], e_tr[:, cc * DC:(cc + 1) * DC, :],
                                   ACT.Copy).then_inc(x0_out, 1)

            def pair_copy(i, c, t, bank):
                wait(act, pairs_made, (i * CH + c) * T0 + (t + 1))
                wait(act, l0_mm, (i * CH + c) * T0 + (t - P_SLOTS + 1))
                act.activation(pairs_hi[0:rows(t), (c * T0 + t) % P_SLOTS, :], bank[0:rows(t), :], ACT.Copy)\
                    .then_inc(pairs_rounded, 1)

            def diag_blocks(i, r, part):
                if part == 0:
                    wait(act, diag_tr, i * 4 + (r + 1))
                    if r == 0 and first(i):
                        wait(act, setup_done, 1)
                    elif r == 0:
                        wait(act, tail_ready, (i - 1) * GU + NG)
                x0 = tr_bank(2, "diag", r)[:, 0:4 * F].rearrange("p (g j) -> p g j", j=F)
                for b in range(4 * part, 4 * part + 4):
                    ins = act.activation(diag[:, 4 * r:4 * r + 4, b, 0:F], x0, ACT.Copy, scale=mask[:, b:b + 1])
                if part == 1:
                    ins.then_inc(diag_made, 1)

            def x1_copies(i, c):
                q = i * CH + c
                wait(act, l0_mm, (q + 1) * T0)
                wait(act, x1_split, q * 2)
                act.activation(x1f[:, :], l0[:, :], ACT.Identity, bias=b0c[:, :]).then_inc(x1_out, 1)
                wait(act, ya_ready, (q - CH + 1) * (DC * HALF))
                act.activation(x1hi[:, c % CH, :], l0[:, :], ACT.Identity, bias=b0c[:, :]).then_inc(x1_out, 1)

            def layer1_bank(i, c, s):
                dd, k = divmod(s, NB)
                u = c * DC + dd
                g = u * HALF + k // 2
                if s < NB and k == 1:
                    wait(act, x0_out, (i * CH + c + 1) * 3)
                wait(act, ya_ready, i * (D * HALF) + g + 1)
                before = g - PROD_SLOTS
                uu, kk = divmod(before, HALF)
                wait(act, prods_added, i * (D * (HALF - 1)) + (uu * (HALF - 1) + max(kk, 1)))
                for j in range(fields(k)):
                    ins = act.activation(prods[:, g % PROD_SLOTS, j * H:(j + 1) * H], ya[g % 2][:, j * H:(j + 1) * H],
                                         ACT.Copy, scale=e_sc[:, u, k * JB + j:k * JB + j + 1])
                ins.then_inc(prods_ready, 1)

            def tail_steps(k, c, s, banks=(tail,)):
                if (c, s - 1) in G_AT:
                    g = G_AT[c, s - 1]
                    wait(act, tail_ready, k * GU + g + 1)
                    act.activation(gram[:, :, 8 * g:8 * g + 8],
                                   banks[g % len(banks)][:, 0:8 * JX].rearrange("p (b j) -> p j b", j=JX), ACT.Copy).then_inc(tail_done, 1)
                if (c, s - 1) == DENSE_AT:
                    wait(act, tail_ready, k * GU + NG + 1)
                    act.activation(dnT[:, :], tail[0:ND, 0:P], ACT.Copy).then_inc(tail_done, 1)
                if (c, s - 2) == max(W2_AT):
                    wait(act, tail_ready, k * GU + NG + 2)
                    act.activation(z2T[:, :], tail[:, 0:P], ACT.Identity, bias=b2sum[:, :]).then_inc(tail_done, 1)
                if (c, s - 2) == TOP1_AT:
                    wait(act, tail_ready, k * GU + NG + 3)
                    for m in range(TOP1 // P):
                        ins = act.activation(h1T[:, m, :], tail[:, m * P:(m + 1) * P], ACT.Relu, bias=bt1[:, m:m + 1])
                    ins.then_inc(tail_done, 1)
                if (c, s - 1) == TOP2_AT:
                    wait(act, tail_ready, k * GU + NG + 4)
                    for m in range(TOP2 // P):
                        ins = act.activation(h2T[:, m, :], tail[:, m * P:(m + 1) * P], ACT.Relu, bias=bt2[:, m:m + 1])
                    ins.then_inc(tail_done, 1)
                if (c, s - 1) == TOP3_AT:
                    wait(act, tail_ready, k * GU + NG + 5)
                    wait(act, y_free, (k + 1) * 16)
                    act.activation(y_sb[:, :], tail[0:1, 0:P], ACT.Copy).then_inc(tail_done, 1)

            weights()
            copy_fields(0)
            for part in range(3):
                x0_copies(0, 0, part, tr[0])
            for t in range(T0):
                pair_copy(0, 0, t, tr[(1 + t) % 2])
            x0_copies(0, 1, 0, tr[0])
            x1_copies(0, 0)
            for part in (1, 2):
                x0_copies(0, 1, part, tr[0])

            def body(i):
                for c in range(CH):
                    ahead = not (last(i) and c == CH - 1)
                    for s in range(SLOTS):
                        if s in S_X0_OUT and not (last(i) and c >= CH - 2):
                            x0_copies(i, c + 2, S_X0_OUT.index(s), tr_bank(c, "x0", 0))
                        if ahead and s == S_X1:
                            x1_copies(i, c + 1)
                        t, off = divmod(s - S_PAIR - 1, EVERY)
                        if ahead and off == 0 and 0 <= t < T0:
                            pair_copy(i, c + 1, t, tr_bank(c, "pair", t))
                        for part, after in enumerate(DIAG_PARTS):
                            if (c, s - after) in DIAG_AT:
                                diag_blocks(i, DIAG_AT[c, s - after], part)
                        if c == 2 and s == S_FIELDS and not last(i):
                            wait(act, x0_tr, (i + 1) * CH)
                            wait(act, x0_out, (i + 1) * (CH * 3))
                            copy_fields(i + 1)
                        if not first(i):
                            tail_steps(i - 1, c, s)
                        if s % 2 == 1:
                            layer1_bank(i, c, s)

            iterations(act, body)
            for c in range(CH):
                for s in range(SLOTS):
                    tail_steps(BT - 1, c, s, idle_banks)

        @block.vector
        def _(dve):
            def pair_products(i, c, t, bank):
                if t == 0:
                    wait(dve, a_loaded, i * (16 * CH) + (c + 1) * 16)
                m = c * T0 + t
                wait(dve, b_loaded[m % B_SLOTS], i * (CH * T0 // B_SLOTS * 16) + (m // B_SLOTS + 1) * 16)
                if c == 0:
                    wait(dve, x0_out, 2 if t == 1 else 0)
                    wait(dve, pairs_split, t - 1)
                else:
                    wait_tr_free(dve, i, c - 1, "pair", t)
                dve.tensor_tensor(bank[0:rows(t), :], x0a[0:rows(t), :], x0s[0:rows(t), m % B_SLOTS, :], ALU.mult)\
                    .then_inc(pairs_made, 1)

            dve.wait_ge(w0_loaded, 16 * 4)
            diagonal = w0x[:, :].rearrange("p (a r) -> p r a", r=FX + 1)
            for s in range(SHIFTS):
                dst = w0s[:, s * F:(s + 1) * F]
                if s == 0:
                    dve.tensor_copy(dst, diagonal[:, 0, :]).then_inc(w0_summed, 1)
                else:
                    other = w0y[:, s * F:s * F + (F + 1) * F].rearrange("p (a r) -> p r a", r=F + 1)[:, 0, :]
                    dve.tensor_tensor(dst, diagonal[:, s, :], other, ALU.add).then_inc(w0_summed, 1)

            banks = yd + ya
            for n, (t, count) in enumerate(((0, 4), (4, T0 - 5), (T0 - 1, 1))):
                bank, at = (banks[0], 0) if n == 0 else (banks[1], t - 4)
                dve.wait_ge(w_hi, min(n, 1) + 1)
                r = rows(t)
                ins = dve.tensor_tensor(w0lo[0:r, t:t + count, :],
                                        bank[0:r, at * P:(at + count) * P].rearrange("p (t h) -> p t h", h=H),
                                        w0hi[0:r, t:t + count, :].bitcast(F32), ALU.subtract)
                if n != 1:
                    ins.then_inc(w_lo, 1)
            for g in range(NB):
                dve.wait_ge(w_hi, 2 + g + 1)
                cols = slice(g * JB * H, (g * JB + fields(g)) * H)
                dve.tensor_tensor(w1lo[:, cols], banks[(2 + g) % 4][:, 0:fields(g) * H],
                                  w1hi[:, cols].bitcast(F32), ALU.subtract).then_inc(w_lo, 1)
            dve.wait_ge(consts_done, 5)
            dve.wait_ge(wtr, 2 + 2 * NB)
            dve.tensor_copy(diag[:, :, :, F], mask[:, :].rearrange("p (o b) -> p o b", o=1).to_broadcast([P, NG, 8]))\
                .then_inc(setup_done, 1)

            def pair_remainder(i, c, t, bank):
                wait(dve, pairs_rounded, (i * CH + c) * T0 + (t + 1))
                r, slot = rows(t), (c * T0 + t) % P_SLOTS
                dve.tensor_tensor(pairs_lo[0:r, slot, :], bank[0:r, :], pairs_hi[0:r, slot, :].bitcast(F32),
                                  ALU.subtract).then_inc(pairs_split, 1)

            def x1_remainder(i, c):
                q = i * CH + c
                wait(dve, x1_out, (q + 1) * 2)
                dve.tensor_tensor(x1lo[:, c % CH, :], x1f[:, :], x1hi[:, c % CH, :].bitcast(F32),
                                  ALU.subtract).then_inc(x1_split, 1)
                wait(dve, z0_done, i + (c // CH))
                dve.tensor_reduce(z0part[:, c % CH, :], x1f[:, :].rearrange("p (d b) -> p b d", b=P),
                                  AX.X, ALU.add).then_inc(x1_split, 1)

            def z0_total(i):
                if not first(i):
                    wait(dve, tail_ready, (i - 1) * GU + NG + 3)
                wait(dve, x1_split, (i + 1) * (2 * CH))
                dve.tensor_reduce(z0T[:, :], z0part[:, :, :].rearrange("p c b -> p b c"), AX.X, ALU.add)\
                    .then_inc(z0_done, 1)

            def layer1_bank(i, c, s):
                dd, k = divmod(s, NB)
                u = c * DC + dd
                g = u * HALF + k // 2
                if s == 0:
                    wait(dve, x0_out, (i * CH + c + 1) * 3)
                wait(dve, yd_ready, i * (D * HALF) + g + 1)
                if k == 0:
                    wait(dve, ab_ready, i * D + (u - 1))
                for j in range(JB):
                    m = (k // 2) * JB + j
                    a = acc[:, u % 2, m % 2, :]
                    y = yd[g % 2][:, j * H:(j + 1) * H]
                    x = e_sc[:, u, k * JB + j:k * JB + j + 1]
                    if m == 0:
                        ins = dve.scalar_tensor_tensor(a, y, x, b1rep[:, :], ALU.mult, ALU.add)
                    elif m == 1:
                        ins = dve.tensor_scalar(a, y, x, None, ALU.mult)
                    else:
                        wait(dve, macs, i * (D * MACS) + (u * MACS + m - 1))
                        ins = dve.scalar_tensor_tensor(a, y, x, a, ALU.mult, ALU.add)
                    ins.then_inc(macs, 1)
                if k == NB - 2:
                    wait(dve, macs, i * (D * MACS) + (u + 1) * MACS)
                    wait(dve, x2_ready, i * D + (u - 1))
                    dve.tensor_tensor(ab[:, u % 2, :], acc[:, u % 2, 0, :], acc[:, u % 2, 1, :], ALU.add)\
                        .then_inc(ab_ready, 1)

            for t in range(T0):
                pair_products(0, 0, t, tr[(1 + t) % 2])
                if t >= 1:
                    pair_remainder(0, 0, t - 1, tr[t % 2])
            pair_remainder(0, 0, T0 - 1, tr[T0 % 2])
            x1_remainder(0, 0)

            def body(i):
                for c in range(CH):
                    ahead = not (last(i) and c == CH - 1)
                    for s in range(SLOTS):
                        t, off = divmod(s - S_PAIR, EVERY)
                        if ahead and off == 0 and 0 <= t < T0:
                            pair_products(i, c + 1, t, tr_bank(c, "pair", t))
                        t, off = divmod(s - S_PAIR - 2, EVERY)
                        if ahead and off == 0 and 0 <= t < T0:
                            pair_remainder(i, c + 1, t, tr_bank(c, "pair", t))
                        if (c, s) == (3, 14):
                            z0_total(i)
                        if ahead and s == S_XL:
                            x1_remainder(i, c + 1)
                        if s % 2 == 0:
                            layer1_bank(i, c, s)

            iterations(dve, body)


def kernel(**inputs):
    import numpy as _np
    import concourse.bacc as _bacc
    from concourse import mybir as _mybir
    from concourse.bass_utils import run_bass_kernel_spmd as _run

    nc = _bacc.Bacc("TRN2", target_bir_lowering=False, num_devices=1)
    arrays, aps = {}, {}
    for name, value in inputs.items():
        a = _np.ascontiguousarray(value)
        arrays[f"in_{name}"] = a
        aps[name] = nc.dram_tensor(f"in_{name}", a.shape, _mybir.dt.from_np(a.dtype), kind="ExternalInput").ap()
    out = nc.dram_tensor("out_y", (B, 1), F32, kind="ExternalOutput").ap()
    cin_tower(nc, aps["dense_ctx"], aps["ids"], [aps[f"tbl_{f}"] for f in range(F)],
              aps["W_top1"], aps["b_top1"], aps["W_top2"], aps["b_top2"], aps["W_top3"],
              aps["L0_rec_W0"], aps["L0_rec_b0"], aps["L0_rec_W1"], aps["L0_rec_b1"],
              aps["L0_rec_W2"], aps["L0_rec_b2"], out)
    r = _run(nc, [arrays], core_ids=[0])
    return r.results[0]["out_y"]
```
